# Optimizing a Trainium2 kernel written in Bass

```python
import numpy as np
import jax
import jax.numpy as jnp

def _softmax(x, axis=-1):
    return jax.nn.softmax(x, axis=axis)

def _gelu(x):
    return jax.nn.gelu(x, approximate=True)

def _silu(x):
    return jax.nn.silu(x)

def _sigmoid(x):
    return jax.nn.sigmoid(x)

def _layernorm(x, axis=-1, eps=1e-05):
    m = jnp.mean(x, axis=axis, keepdims=True)
    v = jnp.var(x, axis=axis, keepdims=True)
    return (x - m) / jnp.sqrt(v + eps)

def _scatter_add(tgt, idx, src, axis=0):
    return tgt.at[idx].add(src)

def _segment_sum(src, seg, n):
    return jax.ops.segment_sum(src, seg, n)
kernel_name = 'mk_macaron_d1_jaxref_r8_02ecc7'

def setup_inputs(seed: int=0):
    np.random.seed(seed)
    _w = jnp.asarray

    def _L0_attn_setup():
        import jax, jax.numpy as jnp
        import numpy as np
        B, S, D_MODEL = (2, 256, 256)
        H, DS, DG, DV = (16, 64, 64, 128)
        ROPE_BASE = 10000.0
        NEG_INF = -1000000000.0

        def _rope(x, base=ROPE_BASE):
            d = x.shape[-1]
            half = d // 2
            inv_freq = 1.0 / base ** (jnp.arange(half, dtype=jnp.float32) / half)
            ang = jnp.arange(x.shape[1], dtype=jnp.float32)[:, None] * inv_freq
            cos = jnp.cos(ang)[None, :, None, :]
            sin = jnp.sin(ang)[None, :, None, :]
            x1, x2 = (x[..., :half], x[..., half:])
            return jnp.concatenate([x1 * cos - x2 * sin, x1 * sin + x2 * cos], axis=-1)
        key = jax.random.key(seed)
        ks = jax.random.split(key, 8)
        s = lambda fan_in: 1.0 / np.sqrt(fan_in)
        return {'x': jax.random.normal(ks[0], (B, S, D_MODEL), dtype=jnp.float32), 'wq_sem': jax.random.normal(ks[1], (D_MODEL, H * DS), dtype=jnp.float32) * s(D_MODEL), 'wk_sem': jax.random.normal(ks[2], (D_MODEL, H * DS), dtype=jnp.float32) * s(D_MODEL), 'wq_geo': jax.random.normal(ks[3], (D_MODEL, H * DG), dtype=jnp.float32) * s(D_MODEL), 'wk_geo': jax.random.normal(ks[4], (D_MODEL, H * DG), dtype=jnp.float32) * s(D_MODEL), 'wv': jax.random.normal(ks[5], (D_MODEL, H * DV), dtype=jnp.float32) * s(D_MODEL), 'wo': jax.random.normal(ks[6], (H * DV, D_MODEL), dtype=jnp.float32) * s(H * DV), 'gate_logit': jax.random.normal(ks[7], (H,), dtype=jnp.float32)}
    _L0_attn_in = _L0_attn_setup()

    def _L0_ffn_setup():
        import jax, jax.numpy as jnp
        import numpy as np
        DIM = 256
        EXPERT_DIM = 128
        N_EXPERTS = 16
        TOPK = 2
        N_SHARED = 1
        B, T = (4, 256)
        key = jax.random.key(seed)
        ks = jax.random.split(key, 9)
        s = 0.02
        return {'x': jax.random.normal(ks[0], (B, T, DIM), jnp.float32), 'router_w': jax.random.normal(ks[1], (N_EXPERTS, DIM), jnp.float32) * s, 'router_bias': jnp.zeros((N_EXPERTS,), jnp.float32), 'Wu': jax.random.normal(ks[2], (N_EXPERTS, DIM, EXPERT_DIM), jnp.float32) * s, 'Wg': jax.random.normal(ks[3], (N_EXPERTS, DIM, EXPERT_DIM), jnp.float32) * s, 'Wd': jax.random.normal(ks[4], (N_EXPERTS, EXPERT_DIM, DIM), jnp.float32) * s, 'Su': jax.random.normal(ks[5], (N_SHARED, DIM, EXPERT_DIM * TOPK), jnp.float32) * s, 'Sg': jax.random.normal(ks[6], (N_SHARED, DIM, EXPERT_DIM * TOPK), jnp.float32) * s, 'Sd': jax.random.normal(ks[7], (N_SHARED, EXPERT_DIM * TOPK, DIM), jnp.float32) * s}
    _L0_ffn_in = _L0_ffn_setup()
    _d = {'L0_attn_x': _L0_attn_in['x'], 'L0_attn_wq_sem': _L0_attn_in['wq_sem'], 'L0_attn_wk_sem': _L0_attn_in['wk_sem'], 'L0_attn_wq_geo': _L0_attn_in['wq_geo'], 'L0_attn_wk_geo': _L0_attn_in['wk_geo'], 'L0_attn_wv': _L0_attn_in['wv'], 'L0_attn_wo': _L0_attn_in['wo'], 'L0_attn_gate_logit': _L0_attn_in['gate_logit'], 'L0_ffn_router_w': _L0_ffn_in['router_w'], 'L0_ffn_router_bias': _L0_ffn_in['router_bias'], 'L0_ffn_Wu': _L0_ffn_in['Wu'], 'L0_ffn_Wg': _L0_ffn_in['Wg'], 'L0_ffn_Wd': _L0_ffn_in['Wd'], 'L0_ffn_Su': _L0_ffn_in['Su'], 'L0_ffn_Sg': _L0_ffn_in['Sg'], 'L0_ffn_Sd': _L0_ffn_in['Sd']}
    _x0 = _d['L0_attn_x']
    _d['L0_attn_x'] = jax.random.normal(jax.random.fold_in(jax.random.key(seed), 1), (1, 1024, 256), dtype=_x0.dtype)
    del _x0
    return _d

def reference(L0_attn_x, L0_attn_wq_sem, L0_attn_wk_sem, L0_attn_wq_geo, L0_attn_wk_geo, L0_attn_wv, L0_attn_wo, L0_attn_gate_logit, L0_ffn_router_w, L0_ffn_router_bias, L0_ffn_Wu, L0_ffn_Wg, L0_ffn_Wd, L0_ffn_Su, L0_ffn_Sg, L0_ffn_Sd):

    def _L0_attn_ref(x, wq_sem, wk_sem, wq_geo, wk_geo, wv, wo, gate_logit):
        import jax, jax.numpy as jnp
        import numpy as np
        B, S, D_MODEL = (2, 256, 256)
        H, DS, DG, DV = (16, 64, 64, 128)
        ROPE_BASE = 10000.0
        NEG_INF = -1000000000.0

        def _rope(x, base=ROPE_BASE):
            d = x.shape[-1]
            half = d // 2
            inv_freq = 1.0 / base ** (jnp.arange(half, dtype=jnp.float32) / half)
            ang = jnp.arange(x.shape[1], dtype=jnp.float32)[:, None] * inv_freq
            cos = jnp.cos(ang)[None, :, None, :]
            sin = jnp.sin(ang)[None, :, None, :]
            x1, x2 = (x[..., :half], x[..., half:])
            return jnp.concatenate([x1 * cos - x2 * sin, x1 * sin + x2 * cos], axis=-1)
        b, sl, _ = x.shape
        qs = (x @ wq_sem).reshape(b, sl, H, DS)
        ksem = (x @ wk_sem).reshape(b, sl, H, DS)
        qg = _rope((x @ wq_geo).reshape(b, sl, H, DG))
        kg = _rope((x @ wk_geo).reshape(b, sl, H, DG))
        v = (x @ wv).reshape(b, sl, H, DV)
        sem_scale = 1.0 / np.sqrt(DS)
        geo_scale = 1.0 / np.sqrt(DG)
        sem_scores = jnp.einsum('bqhd,bkhd->bhqk', qs, ksem) * sem_scale
        geo_scores = jnp.einsum('bqhd,bkhd->bhqk', qg, kg) * geo_scale
        g = jax.nn.sigmoid(gate_logit)[None, :, None, None]
        scores = g * sem_scores + (1.0 - g) * geo_scores
        causal = jnp.tril(jnp.ones((sl, sl), dtype=bool))
        scores = jnp.where(causal[None, None], scores, NEG_INF)
        attn = jax.nn.softmax(scores, axis=-1)
        out = jnp.einsum('bhqk,bkhd->bqhd', attn, v).reshape(b, sl, H * DV)
        return out @ wo

    def _L0_ffn_ref(x, router_w, router_bias, Wu, Wg, Wd, Su, Sg, Sd):
        import jax, jax.numpy as jnp
        import numpy as np
        DIM = 256
        EXPERT_DIM = 128
        N_EXPERTS = 16
        TOPK = 2
        N_SHARED = 1
        B, T = (4, 256)
        Bx, Tx, D = x.shape
        flat = x.reshape(Bx * Tx, D)
        logits = flat @ router_w.T
        scores = jax.nn.softmax(logits, axis=-1)
        _, topk_idx = jax.lax.top_k(logits + router_bias, TOPK)
        topk_scores = jnp.take_along_axis(scores, topk_idx, axis=-1)
        topk_scores = topk_scores / topk_scores.sum(-1, keepdims=True)
        combine = jnp.einsum('nk,nke->ne', topk_scores, jax.nn.one_hot(topk_idx, N_EXPERTS, dtype=scores.dtype))
        out = jnp.zeros_like(flat)
        for e in range(N_EXPERTS):
            h = jax.nn.silu(flat @ Wu[e]) * (flat @ Wg[e])
            out = out + combine[:, e:e + 1] * (h @ Wd[e])
        for s in range(N_SHARED):
            out = out + jax.nn.silu(flat @ Su[s]) * (flat @ Sg[s]) @ Sd[s]
        return out.reshape(Bx, Tx, D)
    x = L0_attn_x
    x = x + 0.5 * _L0_ffn_ref(_layernorm(x, axis=-1), L0_ffn_router_w, L0_ffn_router_bias, L0_ffn_Wu, L0_ffn_Wg, L0_ffn_Wd, L0_ffn_Su, L0_ffn_Sg, L0_ffn_Sd)
    x = x + _L0_attn_ref(_layernorm(x, axis=-1), L0_attn_wq_sem, L0_attn_wk_sem, L0_attn_wq_geo, L0_attn_wk_geo, L0_attn_wv, L0_attn_wo, L0_attn_gate_logit)
    x = x + 0.5 * _L0_ffn_ref(_layernorm(x, axis=-1), L0_ffn_router_w, L0_ffn_router_bias, L0_ffn_Wu, L0_ffn_Wg, L0_ffn_Wd, L0_ffn_Su, L0_ffn_Sg, L0_ffn_Sd)
    return x

_drawn_inputs = setup_inputs


def setup_inputs(seed=0):
    import zlib

    import numpy as np

    out = dict(_drawn_inputs(seed))
    spreads = {'L0_ffn_router_bias': (0.0, 0.8)}
    factors = {'L0_ffn_router_w': 7.325,
     'L0_ffn_Wu': 6.82,
     'L0_ffn_Wg': 6.715,
     'L0_ffn_Wd': 6.685,
     'L0_ffn_Su': 3.397,
     'L0_ffn_Sg': 3.351,
     'L0_ffn_Sd': 3.349}
    for name, (base, spread) in spreads.items():
        noise = np.random.default_rng([zlib.crc32(name.encode()), seed]).standard_normal(out[name].shape)
        drawn = base * np.exp(spread * noise) if base else spread * noise
        out[name] = jnp.asarray(drawn.astype(out[name].dtype))
    for name, factor in factors.items():
        out[name] = (out[name] * factor).astype(out[name].dtype)
    return out
```

```python
from contextlib import ExitStack

import numpy as np

import concourse.bass as bass
from concourse import mybir

ALU = mybir.AluOpType
ACT = mybir.ActivationFunctionType
F32 = mybir.dt.float32
F32R = mybir.dt.float32r
BF16 = mybir.dt.bfloat16
U32 = mybir.dt.uint32
X = mybir.AxisListType.X

P = 128
N, D = 1024, 256
NT, KD = N // P, D // P
HALF = N // 2
LN_EPS = 1e-5

NE, F, TOPK = 16, 128, 2
NSH = 2
NEXP = NSH + NE
RING = 3
TRIPLES = NEXP // RING
WCOLS = 2 * KD * F + D
UNITS = 2 * NEXP

H, DS, DG, DV = 16, 64, 64, 128
HALF_G = DG // 2
GROUPS = H // 2
QT = 4
NEG = 1.0e9
ROPE_BASE = 10000.0
QK_COLS = 4 * P
WQK = KD * QK_COLS
WV = KD * 2 * DV
WO = 2 * D


def wait_apart(engine, sem, value, passed):
    engine.wait_ge(sem, value)
    if not isinstance(value, int):
        engine.sem_inc(passed, 1)


class Names:

    def __init__(self, nc, ctx, prefix):
        self.nc, self.ctx, self.prefix = nc, ctx, prefix

    def sb(self, name, shape, dt=F32):
        return self.ctx.enter_context(self.nc.sbuf_tensor(f"{self.prefix}_{name}", shape, dt))

    def ps(self, name, shape, dt=F32):
        return self.ctx.enter_context(self.nc.psum_tensor(f"{self.prefix}_{name}", shape, dt))

    def sem(self, name):
        return self.ctx.enter_context(self.nc.semaphore(f"{self.prefix}_{name}"))


class Norm:

    def __init__(self, a, x, ident, banks, xn=None):
        self.x, self.ident, self.banks = x, ident, banks
        self.xh = a.sb("xh", [P, KD, N], F32R)
        self.xl = a.sb("xl", [P, KD, N], F32R)
        self.stats = a.sb("stats", [P, NT, 6])
        self.mv = a.sb("mv", [P, NT, 2])
        self.veps = a.sb("veps", [P, NT])
        self.std = a.sb("std", [P, NT])
        self.rstd = a.sb("rstd", [P, NT])
        self.xn = a.sb("xn", [P, 2, D]) if xn is None else xn
        self.stats_done = a.sem("stats_done")
        self.mv_done = a.sem("mv_done")
        self.veps_ready = a.sem("veps_ready")
        self.std_ready = a.sem("std_ready")
        self.rstd_ready = a.sem("rstd_ready")
        self.xn_ready = a.sem("xn_ready")
        self.xt_tile = a.sem("xt_tile")
        self.xhi_ready = a.sem("xhi_ready")
        self.xlo_ready = a.sem("xlo_ready")

    def vector(self, dve):
        for t in range(NT):
            dve.bn_stats(self.stats[:, t, :], self.x[:, t, :]).then_inc(self.stats_done, 1)
        for t in range(NT):
            dve.wait_ge(self.stats_done, t + 1)
            dve.bn_aggr(self.mv[:, t, :], self.stats[:, t, :]).then_inc(self.mv_done, 1)
        dve.wait_ge(self.mv_done, NT)
        dve.tensor_scalar(self.veps[:], self.mv[:, :, 1], LN_EPS, None, ALU.add).then_inc(self.veps_ready, 1)
        dve.wait_ge(self.std_ready, 1)
        dve.reciprocal(self.rstd[:], self.std[:]).then_inc(self.rstd_ready, 1)
        dve.wait_ge(self.rstd_ready, 1)
        for t in range(NT):
            if t >= 2:
                dve.wait_ge(self.xt_tile, t - 1)
            dve.tensor_scalar(self.xn[:, t % 2, :], self.x[:, t, :], self.mv[:, t, 0:1], self.rstd[:, t:t + 1],
                              ALU.subtract, ALU.mult).then_inc(self.xn_ready, 1)
            if t % 4 == 3:
                h = t // 4
                for k in range(KD):
                    b = KD * h + k
                    dve.wait_ge(self.xhi_ready, b + 1)
                    cols = slice(h * HALF, (h + 1) * HALF)
                    dve.tensor_tensor(self.xl[:, k, cols], self.banks[b], self.xh[:, k, cols].bitcast(F32),
                                      ALU.subtract).then_inc(self.xlo_ready, 1)

    def scalar(self, act):
        act.wait_ge(self.veps_ready, 1)
        act.activation(self.std[:], self.veps[:], ACT.Sqrt).then_inc(self.std_ready, 1)
        for b in range(2 * KD):
            h, k = divmod(b, KD)
            act.wait_ge(self.xt_tile, 4 * (h + 1))
            act.activation(self.xh[:, k, h * HALF:(h + 1) * HALF], self.banks[b], ACT.Copy)\
               .then_inc(self.xhi_ready, 1)

    def tensor(self, pe):
        for t in range(NT):
            h, j = divmod(t, 4)
            pe.wait_ge(self.xn_ready, t + 1)
            for k in range(KD):
                last = pe.transpose(self.banks[KD * h + k][:, j * P:(j + 1) * P],
                                    self.xn[:, t % 2, k * P:(k + 1) * P], self.ident[:])
            last.then_inc(self.xt_tile, 1)


def ffn_phase(nc, name, x, consts, w_ffn, w_router, bias, comb_dram, x_in, x_out):
    with ExitStack() as ctx:
        a = Names(nc, ctx, name)
        Y = a.ps("Y", [P, NT, D])
        UG = a.ps("UG", [P, 2, 2, HALF])
        ident, iota = consts[:, 0:P], consts[:, P:P + NE]
        norm = Norm(a, x, ident, [UG[:, b // 2, b % 2, :] for b in range(4)])
        xh, xl = norm.xh, norm.xl

        w_raw = a.sb("w_raw", [P, RING, WCOLS])
        w_hi = a.sb("w_hi", [P, RING, WCOLS], F32R)
        w_lo = a.sb("w_lo", [P, RING, WCOLS], F32R)
        silu = a.sb("silu", [P, 2, HALF])
        hid = a.sb("hid", [P, 2, HALF])
        hid_hi = a.sb("hid_hi", [P, 3, HALF], F32R)
        hid_lo = a.sb("hid_lo", [P, 3, HALF], F32R)
        comb = a.sb("comb", [P, RING, N])

        rw = a.sb("rw", [P, KD * NE])
        rw_hi = a.sb("rw_hi", [P, KD * NE], F32R)
        rw_lo = a.sb("rw_lo", [P, KD * NE], F32R)
        bias_b = a.sb("bias_b", [P, NE])
        logit = a.sb("logit", [P, NT, NE])
        biased = a.sb("biased", [P, NT, NE])
        top = a.sb("top", [P, NT])
        prob = a.sb("prob", [P, NT, NE])
        ssum = a.sb("ssum", [P, NT])
        best = a.sb("best", [P, NT, 8])
        best_at = a.sb("best_at", [P, NT, 8], U32)
        at = a.sb("at", [P, NT, TOPK])
        pick = a.sb("pick", [P, TOPK, NT, NE])
        ksum = a.sb("ksum", [P, NT])
        cw = a.sb("cw", [P, NE, NT])
        cw_t = a.sb("cw_t", [P, P])

        x_loaded = a.sem("x_loaded")
        small_loaded = a.sem("small_loaded")
        w_loaded = [a.sem(f"w_loaded{s}") for s in range(RING)]
        whi_ready = a.sem("whi_ready")
        wlo_ready = a.sem("wlo_ready")
        rw_hi_ready = a.sem("rw_hi_ready")
        rw_ready = a.sem("rw_ready")
        logits_ready = a.sem("logits_ready")
        route = a.sem("route")
        exp_in = a.sem("exp_in")
        exp_ready = a.sem("exp_ready")
        cw_ready = a.sem("cw_ready")
        cwt_ready = a.sem("cwt_ready")
        cwt_copied = a.sem("cwt_copied")
        cw_stored = a.sem("cw_stored")
        comb_loaded = [a.sem(f"comb_loaded{s}") for s in range(RING)]
        ug_ready = a.sem("ug_ready")
        silu_ready = a.sem("silu_ready")
        prod_done = a.sem("prod_done")
        scaled = a.sem("scaled")
        hhi_ready = a.sem("hhi_ready")
        hlo_ready = a.sem("hlo_ready")
        down_done = a.sem("down_done")
        x_updated = a.sem("x_updated")
        stored = a.sem("stored")

        def up(buf, s, k):
            return buf[:, s, k * F:(k + 1) * F]

        def gate(buf, s, k):
            return buf[:, s, (KD + k) * F:(KD + k + 1) * F]

        def down(buf, s):
            return buf[:, s, 2 * KD * F:WCOLS]

        block = ctx.enter_context(nc.Block())

        @block.sync
        def _(sp):
            if x_in is not None:
                sp.dma_start(x[:], x_in.rearrange("(t p) d -> p t d", p=P)).then_inc(x_loaded, 16)
            sp.dma_start(rw[:], w_router).then_inc(small_loaded, 16)
            sp.dma_start(bias_b[:], bias.partition_broadcast(P)).then_inc(small_loaded, 16)
            for e in range(RING):
                sp.dma_start(w_raw[:, e, :], w_ffn[e]).then_inc(w_loaded[e], 16)
            sp.wait_ge(cwt_copied, 1)
            sp.dma_start(comb_dram.rearrange("e (t n) -> (e t) n", t=NT), cw_t[:]).then_inc(cw_stored, 16)
            sp.wait_ge(cw_stored, 16)
            sp.dma_start(comb[:, NSH, :], comb_dram[0].partition_broadcast(P)).then_inc(comb_loaded[NSH], 16)

            def loads(g, s):
                e = RING * g + s
                sp.wait_ge(wlo_ready, e - 2)
                sp.dma_start(w_raw[:, s, :], w_ffn[bass.ds(e, 1)].rearrange("e p n -> p (e n)"))\
                  .then_inc(w_loaded[s], 16)
                if s < NSH:
                    sp.wait_ge(prod_done, 2 * e - 4)
                sp.wait_ge(hlo_ready, 2 * e - 4)
                sp.dma_start(comb[:, s, :], comb_dram[bass.ds(e - NSH, 1)].rearrange("e n -> (e n)")
                             .partition_broadcast(P)).then_inc(comb_loaded[s], 16)

            with sp.Fori(1, TRIPLES) as g:
                for s in range(RING):
                    loads(g, s)
            if x_out is not None:
                out_v = x_out.rearrange("(b t p) d -> b p t d", p=P, t=2)
                for b in range(NT // 2):
                    sp.wait_ge(x_updated, b + 1)
                    sp.dma_start(out_v[b], x[:, 2 * b:2 * b + 2, :]).then_inc(stored, 16)
                sp.wait_ge(stored, 16 * (NT // 2))
            sp.wait_ge(cw_stored, 16)

        @block.gpsimd
        def _(pool):
            with pool.Fori(0, TRIPLES) as g:
                for s in range(RING):
                    pool.wait_ge(whi_ready, RING * g + s + 1)
                    pool.tensor_tensor(w_lo[:, s, :], w_raw[:, s, :], w_hi[:, s, :].bitcast(F32), ALU.subtract)\
                        .then_inc(wlo_ready, 1)

        @block.scalar
        def _(act):
            def split_weights(g, s):
                e = RING * g + s
                act.wait_ge(w_loaded[s], 16 * (g + 1))
                if not isinstance(e, int) or e >= RING:
                    act.wait_ge(down_done, 2 * e - 4)
                act.activation(w_hi[:, s, :], w_raw[:, s, :], ACT.Copy).then_inc(whi_ready, 1)

            def expert(g, s, shared, more):
                for half in range(2):
                    n = 2 * (RING * g + s) + half
                    act.wait_ge(ug_ready, n + 1)
                    act.activation(silu[:, half, :], UG[:, half, 0, :], ACT.Silu).then_inc(silu_ready, 1)
                    if shared:
                        act.wait_ge(prod_done, n + 1)
                    else:
                        act.wait_ge(scaled, n + 1 - 2 * NSH)
                    r = (2 * s + half) % 3
                    if not isinstance(n, int) or n >= 3:
                        act.wait_ge(down_done, n - 2)
                    act.activation(hid_hi[:, r, :], hid[:, half, :], ACT.Copy).then_inc(hhi_ready, 1)
                    if half == 0 and more:
                        split_weights(g + (s + 1) // RING, (s + 1) % RING)

            norm.scalar(act)
            split_weights(0, 0)
            act.wait_ge(exp_in, 1)
            act.activation(prob[:], prob[:], ACT.Exp).then_inc(exp_ready, 1)
            for s in range(RING):
                expert(0, s, s < NSH, True)
            with act.Fori(1, TRIPLES - 1) as g:
                for s in range(RING):
                    expert(g, s, False, True)
            for s in range(RING):
                expert(TRIPLES - 1, s, False, s < RING - 1)

        @block.vector
        def _(dve):
            if x_in is not None:
                dve.wait_ge(x_loaded, 16)
            norm.vector(dve)
            dve.wait_ge(small_loaded, 32)
            dve.tensor_copy(rw_hi[:], rw[:]).then_inc(rw_hi_ready, 1)
            dve.wait_ge(rw_hi_ready, 1)
            dve.tensor_tensor(rw_lo[:], rw[:], rw_hi[:].bitcast(F32), ALU.subtract).then_inc(rw_ready, 1)

            steps = [0]

            def step(instruction):
                instruction.then_inc(route, 1)
                steps[0] += 1
                dve.wait_ge(route, steps[0])

            def over_experts(v):
                return v.unsqueeze(2).broadcast_to([P, NT, NE])

            dve.wait_ge(logits_ready, 1)
            step(dve.tensor_copy(logit[:], Y[:, NT - 1, 0:NT * NE].rearrange("p (t e) -> p t e", e=NE)))
            step(dve.tensor_reduce(top[:], logit[:], X, ALU.max))
            dve.tensor_tensor(prob[:], logit[:], over_experts(top[:]), ALU.subtract).then_inc(exp_in, 1)
            step(dve.tensor_tensor(biased[:], logit[:], bias_b[:].unsqueeze(1).broadcast_to([P, NT, NE]), ALU.add))
            for t in range(NT):
                last = dve.max(best[:, t, :], biased[:, t, :])
            step(last)
            for t in range(NT):
                last = dve.max_index(best_at[:, t, :], best[:, t, :], biased[:, t, :])
            step(last)
            step(dve.tensor_copy(at[:], best_at[:, :, 0:TOPK]))
            for k in range(TOPK):
                last = dve.tensor_tensor(pick[:, k, :, :], iota.unsqueeze(1).broadcast_to([P, NT, NE]),
                                         over_experts(at[:, :, k]), ALU.is_equal)
            step(last)
            step(dve.tensor_tensor(pick[:, 0, :, :], pick[:, 0, :, :], pick[:, 1, :, :], ALU.add))
            dve.wait_ge(exp_ready, 1)
            step(dve.tensor_reduce(ssum[:], prob[:], X, ALU.add))
            step(dve.reciprocal(ssum[:], ssum[:]))
            step(dve.tensor_tensor(prob[:], prob[:], over_experts(ssum[:]), ALU.mult))
            step(dve.tensor_tensor(prob[:], prob[:], pick[:, 0, :, :], ALU.mult))
            step(dve.tensor_reduce(ksum[:], prob[:], X, ALU.add))
            step(dve.reciprocal(ksum[:], ksum[:]))
            dve.tensor_tensor(cw[:].rearrange("p e t -> p t e"), prob[:], over_experts(ksum[:]), ALU.mult)\
               .then_inc(cw_ready, 1)

            def expert(g, s, shared, first):
                for half in range(2):
                    e = RING * g + s
                    n = 2 * e + half
                    if first and n == 3:
                        dve.wait_ge(cwt_ready, 1)
                        dve.tensor_copy(cw_t[:], UG[:, 1, 0, 0:P]).then_inc(cwt_copied, 1)
                    dve.wait_ge(silu_ready, n + 1)
                    dve.tensor_tensor(hid[:, half, :], UG[:, half, 1, :], silu[:, half, :], ALU.mult)\
                       .then_inc(prod_done, 1)
                    if not shared:
                        dve.wait_ge(prod_done, n + 1)
                        if half == 0:
                            dve.wait_ge(comb_loaded[s], 16 * (g + s // NSH))
                        dve.tensor_tensor(hid[:, half, :], hid[:, half, :],
                                          comb[:, s, half * HALF:(half + 1) * HALF], ALU.mult).then_inc(scaled, 1)
                    r = (2 * s + half) % 3
                    dve.wait_ge(hhi_ready, n + 1)
                    dve.tensor_tensor(hid_lo[:, r, :], hid[:, half, :], hid_hi[:, r, :].bitcast(F32), ALU.subtract)\
                       .then_inc(hlo_ready, 1)

            for s in range(RING):
                expert(0, s, s < NSH, True)
            with dve.Fori(1, TRIPLES) as g:
                for s in range(RING):
                    expert(g, s, False, False)
            for b in range(NT // 2):
                dve.wait_ge(down_done, UNITS - 1 + b // 2)
                dve.scalar_tensor_tensor(x[:, 2 * b:2 * b + 2, :].rearrange("p t d -> p (t d)"),
                                         Y[:, 2 * b:2 * b + 2, :].rearrange("p t d -> p (t d)"), 0.5,
                                         x[:, 2 * b:2 * b + 2, :].rearrange("p t d -> p (t d)"),
                                         ALU.mult, ALU.add).then_inc(x_updated, 1)

        @block.tensor
        def _(pe):
            norm.tensor(pe)
            pe.wait_ge(norm.xlo_ready, 4)
            pe.wait_ge(rw_ready, 1)
            logits = Y[:, NT - 1, 0:NT * NE]
            for t in range(NT):
                at_t = logits[:, t * NE:(t + 1) * NE]
                for k in range(KD):
                    cols, rk = slice(t * P, (t + 1) * P), slice(k * NE, (k + 1) * NE)
                    pe.matmul(at_t, xh[:, k, cols], rw_hi[:, rk], start=(k == 0), stop=False)
                    pe.matmul(at_t, xh[:, k, cols], rw_lo[:, rk], start=False, stop=False)
                    last = pe.matmul(at_t, xl[:, k, cols], rw_hi[:, rk], start=False, stop=(k == KD - 1))
            last.then_inc(logits_ready, 1)

            def up_gate(s, half):
                cols = slice(half * HALF, (half + 1) * HALF)
                for which, part in ((0, up), (1, gate)):
                    out = UG[:, half, which, :]
                    for k in range(KD):
                        pe.matmul(out, part(w_hi, s, k), xh[:, k, cols], start=(k == 0), stop=False)
                        pe.matmul(out, part(w_hi, s, k), xl[:, k, cols], start=False, stop=False)
                        last = pe.matmul(out, part(w_lo, s, k), xh[:, k, cols], start=False, stop=(k == KD - 1))
                last.then_inc(ug_ready, 1)

            def project_down(n, s, half, first, final):
                pe.wait_ge(hlo_ready, n + 1)
                r = (2 * s + half) % 3
                for j in range(4):
                    out, cols = Y[:, 4 * half + j, :], slice(j * P, (j + 1) * P)
                    pe.matmul(out, hid_hi[:, r, cols], down(w_hi, s), start=(first and j % 2 == 0), stop=False,
                              skip_group_check=True)
                    pe.matmul(out, hid_hi[:, r, cols], down(w_lo, s), start=False, stop=False, skip_group_check=True)
                    last = pe.matmul(out, hid_lo[:, r, cols], down(w_hi, s), start=False,
                                     stop=(final and j % 2 == 1), skip_group_check=True)
                last.then_inc(down_done, 1)

            def expert(g, s, first):
                e = RING * g + s
                pe.wait_ge(wlo_ready, e + 1)
                for half in range(2):
                    n = 2 * e + half
                    if first and n == 3:
                        pe.wait_ge(prod_done, n - 1)
                        pe.wait_ge(cw_ready, 1)
                        pe.transpose(UG[:, 1, 0, 0:P], cw[:].rearrange("p e t -> p (e t)"), ident[:])\
                          .then_inc(cwt_ready, 1)
                        pe.wait_ge(cwt_copied, 1)
                    elif not first or n >= 2:
                        pe.wait_ge(prod_done, n - 1)
                    up_gate(s, half)
                    if not first or n >= 2:
                        project_down(n - 2, (s - 1) % RING, half, first and s == 1, False)

            for s in range(RING):
                expert(0, s, True)
            with pe.Fori(1, TRIPLES) as g:
                for s in range(RING):
                    expert(g, s, False)
            for half in range(2):
                project_down(UNITS - 2 + half, RING - 1, half, False, True)



DIAG = 3 * P
DIAG_COLS = 3 * DIAG + QT * P
PT_COLS = 2 * DIAG_COLS + QT * QT * P
LO, HI = 0, 1

P_SLOT = [(0, P), (P, 2 * P), (3 * P, 6 * P), (9 * P, 7 * P), (16 * P, 8 * P),
          (3 * P, 6 * P), (9 * P, 7 * P), (16 * P, 8 * P)]
P_COLS = 24 * P
BATCH = [0, 1, 2, 3, 4, 6, 8, 10]
BATCHES = 12

BESIDE = {
    (0, 0): ([("X", 0, 0)], [("X", 0, 1)]),
    (0, 1): ([("PV", -1)], []),
    (0, 2): ([("W", -1, 0)], [("W", -1, 1)]),
    (0, 3): ([("V", 0)], [("V", 1)]),
    (0, 4): ([("V", 2)], [("V", 3), ("G", 0)]),
    (0, 5): ([("S", 0, 0)], [("PV", 0)]),
    (0, 6): ([("X", 1, 0)], [("X", 1, 1)]),
    (0, 7): ([("W", 0, 0)], [("W", 0, 1)]),
    (1, 0): ([("S", 0, 1)], []),
    (1, 1): ([("PV", 1)], []),
    (1, 2): ([("W", 1, 0)], [("W", 1, 1)]),
    (1, 3): ([("S", 1, 0)], [("G", 1)]),
    (1, 4): ([("S", 1, 1)], []),
    (1, 5): ([], [("PV", 2)]),
    (1, 6): ([("W", 2, 0)], []),
    (1, 7): ([("W", 2, 1)], []),
}
ROPE_OPS = {(0, 1): (0, 0, 2), (0, 2): (0, 2, 4), (0, 3): (0, 4, 6),
            (0, 7): (1, 0, 1), (1, 0): (1, 1, 3), (1, 1): (1, 3, 5), (1, 2): (1, 5, 6)}
PRO = [("X", 0, 0), ("X", 0, 1), ("G", 0), ("S", 0, 0), ("S", 0, 1), ("X", 1, 0), ("X", 1, 1), ("S", 1, 0), ("S", 1, 1), ("G", 1)]


def chunks(first, last):
    order = [t for step in sorted(BESIDE) for part in BESIDE[step] for t in part]
    return [t for t in order if t[0] in "XSVW" and not absent(t, first, last)]


def absent(task, first, last):
    return (first and task[0] in ("PV", "W") and task[1] == -1) or (last and task[0] in ("X", "S", "G"))


PRO_CHUNKS = [t for t in PRO if t[0] != "G"]
FULL = len(chunks(False, False))


def group_base(g, first):
    return len(PRO_CHUNKS) if first else FULL * g + len(PRO_CHUNKS) + len(chunks(True, False)) - FULL


def chunk_index(g, task, first, last):
    return group_base(g, first) + chunks(first, last).index(task)


def ring(first, last):
    order = [t for step in sorted(BESIDE) for part in BESIDE[step] for t in part]
    return [t for t in order if t[0] != "G" and not absent(t, first, last)]


RING_FULL = ring(False, False)
RING_BASE = len(PRO_CHUNKS) + len(ring(True, False)) - len(RING_FULL)


def bank_of(task, first, last):
    return ((len(PRO_CHUNKS) if first else RING_BASE) + ring(first, last).index(task)) % 2


def read_index(g, task, first, last):
    kind = task[0] == "X"
    done, mine, full = ([t for t in tasks if (t[0] == "X") == kind]
                        for tasks in (PRO_CHUNKS, ring(first, last), RING_FULL))
    if first:
        return len(done) + mine.index(task)
    before = [t for t in ring(True, False) if (t[0] == "X") == kind]
    return len(full) * g + len(done) + len(before) - len(full) + mine.index(task)


def bank_reader(g, task, first, last):
    order = ring(first, last)
    at = order.index(task) - 2
    if at >= 0:
        return order[at][0] == "X", read_index(g, order[at], first, last)
    if first:
        old = PRO_CHUNKS[at]
        kind = old[0] == "X"
        return kind, [t for t in PRO_CHUNKS if (t[0] == "X") == kind].index(old)
    old = RING_FULL[at]
    kind = old[0] == "X"
    mine = [t for t in RING_FULL if (t[0] == "X") == kind]
    first_of_kind = next(t for t in RING_FULL if (t[0] == "X") == kind)
    return kind, read_index(g, first_of_kind, False, False) - (len(mine) - mine.index(old))


def split_index(g, task, first, last):
    mine = [t for t in chunks(first, last) if t[0] in "VS"]
    return 4 + 8 * g + mine.index(task)


def attention_phase(nc, name, x, consts, w_qk, w_v, w_o, gate, rope):
    with ExitStack() as ctx:
        a = Names(nc, ctx, name)
        S = a.ps("S", [P, 4, HALF])
        TR = a.ps("TR", [P, 2, QT, P])
        M = a.ps("M", [P, 2, HALF])
        ident = consts[:, 0:P]

        probs = a.sb("probs", [P, P_COLS])
        norm = Norm(a, x, ident, [S[:, b, :] for b in range(4)], probs[:, 0:2 * D].rearrange("p (t d) -> p t d", t=2))
        xh, xl = norm.xh, norm.xl
        qk = a.sb("qk", [P, 2, 2, 2, 2, N], F32R)
        v = a.sb("v", [P, 2, NT, 2 * DV], F32R)
        pt = a.sb("pt", [P, 2, PT_COLS], F32R)
        ot = a.sb("ot", [P, 2, HALF], F32R)
        raw_qk = a.sb("raw_qk", [P, WQK])
        raw_vo = a.sb("raw_vo", [P, WV])
        wqk = a.sb("wqk", [P, 2, WQK], F32R)
        wv = a.sb("wv", [P, 2, WV], F32R)
        wo = a.sb("wo", [P, 2, WO], F32R)
        cs = a.sb("cs", [P, 2, N])
        rot = a.sb("rot", [P, 4, HALF])
        x2 = a.sb("x2", [P, HALF])
        x2s = a.sb("x2s", [P, HALF])
        mask = a.sb("mask", [P, N], BF16)
        s_sem = a.sb("s_sem", [P, GROUPS])
        s_geo = a.sb("s_geo", [P, GROUPS])
        low = a.sb("low", [P, 4])
        total = a.sb("total", [P, 4])
        inv = a.sb("inv", [P, 4])

        tables_loaded = a.sem("tables_loaded")
        gate_loaded = a.sem("gate_loaded")
        gate_sig = a.sem("gate_sig")
        gate_ready = a.sem("gate_ready")
        passed_pool = a.sem("passed_pool")
        passed_act = a.sem("passed_act")
        passed_dve = a.sem("passed_dve")
        pt_zero = a.sem("pt_zero")
        mask_zero = a.sem("mask_zero")
        mask_ready = a.sem("mask_ready")
        qk_loaded = a.sem("qk_loaded")
        v_loaded = a.sem("v_loaded")
        o_loaded = a.sem("o_loaded")
        wqk_hi = a.sem("wqk_hi")
        wv_hi = a.sem("wv_hi")
        wo_hi = a.sem("wo_hi")
        wqk_lo = a.sem("wqk_lo")
        wv_lo = a.sem("wv_lo")
        wo_lo = a.sem("wo_lo")
        m_ready = a.sem("m_ready")
        x_read = a.sem("x_read")
        m_read = a.sem("m_read")
        m_hi = a.sem("m_hi")
        rope_step = a.sem("rope_step")
        geo_hi = a.sem("geo_hi")
        geo_lo = a.sem("geo_lo")
        geo_moved = a.sem("geo_moved")
        s_ready = a.sem("s_ready")
        low_ready = a.sem("low_ready")
        exp_done = a.sem("exp_done")
        inv_ready = a.sem("inv_ready")
        probs_ready = a.sem("probs_ready")
        tr_ready = a.sem("tr_ready")
        pt_hi = a.sem("pt_hi")
        pt_lo = a.sem("pt_lo")
        pv_done = a.sem("pv_done")
        ot_hi = a.sem("ot_hi")

        MOVES = 8 * 16

        def tile_of(g, hh, i):
            return 2 * NT * g + NT * hh + i

        def batch_of(g, hh, i):
            return 2 * BATCHES * g + BATCHES * hh + BATCH[i]

        def probs_of(i, n):
            at, _ = P_SLOT[i]
            return probs[:, at:at + n]

        def scores_of(i, n):
            at = i * HALF if i < 4 else (i % 2) * N
            return S[:].rearrange("p b n -> p (b n)")[:, at:at + n]

        def pt_col(G, kt, qj):
            base = G * DIAG_COLS
            if kt < QT * G:
                return base + kt * QT * P + qj * P
            return base + QT * P * QT * G + (kt - QT * G) * DIAG + qj * P

        def pt_cells(part, G, kt0, n, qj):
            stride = QT * P if kt0 < QT * G else DIAG
            at = pt_col(G, kt0, qj)
            if n == 1:
                return pt[:, part, at:at + P].unsqueeze(1)
            return pt[:, part, at:at + n * stride].rearrange("p (k n) -> p k n", n=stride)[:, :, 0:P] \
                if at + n * stride <= PT_COLS else tail_cells(part, at, n, stride)

        def tail_cells(part, at, n, stride):
            shift = at + n * stride - PT_COLS
            return pt[:, part, at - shift:PT_COLS].rearrange("p (k n) -> p k n", n=stride)[:, :, shift:shift + P]

        def batches(i):
            return [(QT * c, min(QT, i + 1 - QT * c)) for c in range(i // QT + 1)]

        def ahead(hh, i, group, last):
            if i + 2 < NT:
                return group, hh, i + 2
            if hh == 0:
                return group, 1, i + 2 - NT
            return None if last else (group + 1, 0, i + 2 - NT)

        END_BANK = (bank_of(("W", 2, 1), False, True) + 1) % 2

        block = ctx.enter_context(nc.Block())

        @block.sync
        def _(sp):
            def load_qk(g):
                sp.dma_start(raw_qk[:], w_qk[bass.ds(g, 1)].rearrange("g p n -> p (g n)")).then_inc(qk_loaded, 16)

            def load_v(g):
                sp.dma_start(raw_vo[:], w_v[bass.ds(g, 1)].rearrange("g p n -> p (g n)")).then_inc(v_loaded, 16)

            def load_o(g):
                sp.dma_start(raw_vo[:], w_o[bass.ds(g, 1)].rearrange("g p n -> p (g n)")).then_inc(o_loaded, 16)

            def move_geo(g, par, half):
                sp.wait_ge(geo_lo, 2 * (2 * g + half + 1))
                cols = slice(half * HALF, (half + 1) * HALF)
                for which in range(2):
                    for block_ in range(4):
                        is_k, hh = divmod(block_, 2)
                        to = HALF_G * which + (DS if hh == 0 else 0)
                        sp.dma_start(qk[to:to + HALF_G, par, is_k, hh, :, cols].bitcast(F32),
                                     rot[HALF_G * block_:HALF_G * (block_ + 1), 2 * which:2 * which + 2, :])\
                          .then_inc(geo_moved, 16)

            load_qk(0)
            for b in range(2):
                sp.dma_start(s_sem[b * DS:(b + 1) * DS, :], gate[b].partition_broadcast(DS)).then_inc(gate_loaded, 16)
                sp.dma_start(s_geo[b * HALF_G:(b + 1) * HALF_G, :], gate[b].partition_broadcast(HALF_G))\
                  .then_inc(gate_loaded, 16)
            load_v(0)
            sp.dma_start(cs[:], rope).then_inc(tables_loaded, 16)
            sp.wait_ge(wqk_lo, 1)
            load_qk(1)
            sp.wait_ge(wv_lo, 1)
            load_o(0)
            for half in range(2):
                move_geo(0, 0, half)

            def group(g, par, last):
                if not last:
                    sp.wait_ge(wqk_lo, g + 2)
                    load_qk(g + 2)
                    move_geo(g + 1, 1 - par, 0)
                    sp.wait_ge(wo_lo, g + 1)
                    load_v(g + 1)
                    move_geo(g + 1, 1 - par, 1)
                    sp.wait_ge(wv_lo, g + 2)
                    load_o(g + 1)

            group(0, 0, False)
            with sp.Fori(0, (GROUPS - 2) // 2) as i:
                group(2 * i + 1, 1, False)
                group(2 * i + 2, 0, False)
            group(GROUPS - 1, 1, True)

        @block.gpsimd
        def _(pool):
            def split(sem, done, n, lo, raw, hi):
                pool.wait_ge(sem, n)
                pool.tensor_tensor(lo, raw, hi.bitcast(F32), ALU.subtract).then_inc(done, 1)

            def rope_ops(r, half, start, stop):
                cols = slice(half * HALF, (half + 1) * HALF)
                cos, sin = cs[:, 0, cols], cs[:, 1, cols]
                o1, x1 = rot[:, 0, :], rot[:, 2, :]
                for k in range(start, stop):
                    if k == 0:
                        pool.wait_ge(x_read, 2 * r + 2)
                        op = pool.tensor_tensor(o1, x1, cos, ALU.mult)
                    if k == 1:
                        op = pool.tensor_tensor(x2s[:], x2[:], sin, ALU.mult)
                    if k == 2:
                        pool.wait_ge(rope_step, 6 * r + 2)
                        op = pool.tensor_tensor(o1, o1, x2s[:], ALU.subtract)
                    if k == 3:
                        op = pool.tensor_tensor(x1, x1, sin, ALU.mult)
                    if k == 4:
                        op = pool.tensor_tensor(x2[:], x2[:], cos, ALU.mult)
                    if k == 5:
                        pool.wait_ge(rope_step, 6 * r + 5)
                        op = pool.tensor_tensor(x1, x1, x2[:], ALU.add)
                    op.then_inc(rope_step, 1)

            def normalize(tile):
                g, hh, i = tile
                T = tile_of(g, hh, i)
                wait_apart(pool, inv_ready, T + 1, passed_pool)
                row = probs_of(i, (i + 1) * P)
                pool.tensor_scalar(row, row, inv[:, i % 4:i % 4 + 1], 1.0, ALU.mult, ALU.mult)\
                    .then_inc(probs_ready, 1)

            pool.memset(mask[:], 0.0).then_inc(mask_zero, 1)
            for part in (LO, HI):
                for G in range(2):
                    at = pt_col(G, QT * G + 3, 2)
                    pool.memset(pt[:, part, at:at + P].bitcast(F32), 0.0).then_inc(pt_zero, 1)
            pool.wait_ge(mask_zero, 1)
            pool.affine_select(out=mask[:, N - P:N], in_=mask[:, N - P:N], compare_op=ALU.is_ge, fill=NEG,
                               base=0, pattern=[[-1, P]], channel_multiplier=1).then_inc(mask_ready, 1)
            split(wqk_hi, wqk_lo, 1, wqk[:, LO, :], raw_qk[:], wqk[:, HI, :])
            split(wv_hi, wv_lo, 1, wv[:, LO, :], raw_vo[:], wv[:, HI, :])
            pool.wait_ge(tables_loaded, 16)
            for half in range(2):
                rope_ops(half, half, 0, 6)
            split(wqk_hi, wqk_lo, 2, wqk[:, LO, :], raw_qk[:], wqk[:, HI, :])
            for i in range(2):
                normalize((0, 0, i))

            def group(g, par, first, last):
                for hh in range(2):
                    for i in range(NT):
                        tile = ahead(hh, i, g, last)
                        if tile is not None:
                            normalize(tile)
                        if not last and (hh, i) in ROPE_OPS:
                            half, start, stop = ROPE_OPS[hh, i]
                            rope_ops(2 * g + 2 + half, half, start, stop)
                        if (hh, i) == (0, 3):
                            split(wo_hi, wo_lo, g + 1, wo[:, LO, :], raw_vo[:], wo[:, HI, :])
                        if (hh, i) == (1, 5) and not last:
                            split(wqk_hi, wqk_lo, g + 3, wqk[:, LO, :], raw_qk[:], wqk[:, HI, :])
                            split(wv_hi, wv_lo, g + 2, wv[:, LO, :], raw_vo[:], wv[:, HI, :])

            group(0, 0, True, False)
            with pool.Fori(0, (GROUPS - 2) // 2) as j:
                group(2 * j + 1, 1, False, False)
                group(2 * j + 2, 0, False, False)
            group(GROUPS - 1, 1, False, True)

        @block.scalar
        def _(act):
            def exps(tile):
                g, hh, i = tile
                T = tile_of(g, hh, i)
                act.wait_ge(low_ready, T + 1)
                if not isinstance(T, int) or T >= 3:
                    j = (i - 3) % NT
                    act.wait_ge(tr_ready, batch_of(g, hh, j) + len(batches(j)) - (BATCHES if i < 3 else 0))
                n = (i + 1) * P
                act.activation(probs_of(i, n), scores_of(i, n), ACT.Exp, bias=low[:, i % 4:i % 4 + 1], scale=-1.0,
                               accum_out=total[:, i % 4:i % 4 + 1]).then_inc(exp_done, 1)

            def round_transposed(g, hh, i):
                for c, (kt0, n) in enumerate(batches(i)):
                    b = batch_of(g, hh, i) + c
                    act.wait_ge(tr_ready, b + 1)
                    if c == 0 and i % QT == 0 and (not isinstance(g, int) or 4 * g + 2 * hh + i // QT >= 2):
                        act.wait_ge(pv_done, 4 * g + 2 * hh + i // QT - 1)
                    act.activation(pt_cells(HI, i // QT, kt0, n, i % QT), TR[:, (BATCH[i] + c) % 2, 0:n, :], ACT.Copy)\
                       .then_inc(pt_hi, 1)

            def task(t, g, par, first, last, m, bank):
                proj = M[:, bank, :] if bank is not None else None
                if t[0] == "X":
                    _, half, which = t
                    if not isinstance(g, int) or 2 * g + half > 0:
                        act.wait_ge(geo_moved, MOVES * (2 * g + half))
                    wait_apart(act, m_ready, m + 1, passed_act)
                    act.activation(rot[:, 2, :] if which == 0 else x2[:], proj, ACT.Copy,
                                   scale=s_geo[:, bass.ds(g, 1)]).then_inc(x_read, 1)
                if t[0] == "S":
                    _, is_k, half = t
                    wait_apart(act, m_ready, m + 1, passed_act)
                    for hh in range(2):
                        rows = slice(hh * DS, (hh + 1) * DS)
                        out = qk[rows, par, is_k, hh, HI, half * HALF:(half + 1) * HALF]
                        if is_k:
                            op = act.activation(out, proj[rows, :], ACT.Copy)
                        else:
                            op = act.activation(out, proj[rows, :], ACT.Copy, scale=s_sem[rows, bass.ds(g, 1)])
                    op.then_inc(m_hi, 1)
                if t[0] == "G":
                    r = 2 * g + t[1]
                    for which in range(2):
                        act.wait_ge(rope_step, 6 * r + 3 * (which + 1))
                        act.activation(rot[:, 2 * which + 1, :].bitcast(F32R), rot[:, 2 * which, :], ACT.Copy)\
                           .then_inc(geo_hi, 1)
                if t[0] == "V":
                    c = t[1]
                    act.wait_ge(m_ready, m + 1)
                    if c == 0 and not first:
                        act.wait_ge(pv_done, 4 * g)
                    act.activation(v[:, HI, 2 * c:2 * c + 2, :].rearrange("p t n -> p (t n)"), proj, ACT.Copy)\
                       .then_inc(m_hi, 1)
                if t[0] == "PV":
                    u = 4 * g + t[1]
                    act.wait_ge(pv_done, u + 1)
                    if not (first and t[1] == 0):
                        act.wait_ge(m_ready, m)
                    act.activation(ot[:, HI, :], proj, ACT.Copy).then_inc(ot_hi, 1)

            def split(sem, n, done, hi, raw, after=None):
                act.wait_ge(sem, 16 * n)
                if after is not None:
                    act.wait_ge(m_ready, after)
                act.activation(hi, raw, ACT.Copy).then_inc(done, 1)

            norm.scalar(act)
            act.wait_ge(gate_loaded, 64)
            act.activation(s_sem[:], s_sem[:], ACT.Sigmoid).then_inc(gate_sig, 1)
            act.activation(s_geo[0:2 * HALF_G, :], s_geo[0:2 * HALF_G, :], ACT.Sigmoid).then_inc(gate_sig, 1)
            split(qk_loaded, 1, wqk_hi, wqk[:, HI, :], raw_qk[:])
            split(v_loaded, 1, wv_hi, wv[:, HI, :], raw_vo[:])
            act.wait_ge(gate_ready, 1)
            for t in PRO:
                m = PRO_CHUNKS.index(t) if t in PRO_CHUNKS else None
                task(t, 0, 0, True, False, m, m % 2 if m is not None else None)
            split(qk_loaded, 2, wqk_hi, wqk[:, HI, :], raw_qk[:], len(PRO_CHUNKS))
            for i in range(2):
                exps((0, 0, i))

            def group(g, par, first, last):
                def beside(tasks):
                    for t in tasks:
                        if absent(t, first, last):
                            continue
                        nxt = t[0] in "XSG"
                        if t[0] in ("X", "S", "V"):
                            m = chunk_index(g, t, first, last)
                        elif t[0] == "PV" and not (first and t[1] == 0):
                            m = chunk_index(g, ("W", t[1] - 1, 1), first, last) + 1 if t[1] >= 0 else \
                                group_base(g, first)
                        else:
                            m = None
                        bank = None if t[0] == "G" else bank_of(t, first, last)
                        task(t, g + 1 if nxt else g, 1 - par if nxt else par, first, last, m, bank)

                for hh in range(2):
                    for i in range(NT):
                        tile = ahead(hh, i, g, last)
                        before = BESIDE[hh, i][0]
                        long = any(t[0] == "PV" for t in before)
                        if tile is not None and long:
                            exps(tile)
                        beside(before)
                        round_transposed(g, hh, i)
                        if tile is not None and not long:
                            exps(tile)
                        beside(BESIDE[hh, i][1])
                        if (hh, i) == (0, 3):
                            after = None if first else chunk_index(g, ("W", -1, 1), first, last) + 1
                            split(o_loaded, g + 1, wo_hi, wo[:, HI, :], raw_vo[:], after)
                        if (hh, i) == (1, 5) and not last:
                            split(qk_loaded, g + 3, wqk_hi, wqk[:, HI, :], raw_qk[:],
                                  chunk_index(g, ("S", 1, 1), first, last) + 1)
                            split(v_loaded, g + 2, wv_hi, wv[:, HI, :], raw_vo[:])

            group(0, 0, True, False)
            with act.Fori(0, (GROUPS - 2) // 2) as j:
                group(2 * j + 1, 1, False, False)
                group(2 * j + 2, 0, False, False)
            group(GROUPS - 1, 1, False, True)
            m_end = chunk_index(GROUPS - 1, ("W", 2, 1), False, True) + 1
            act.wait_ge(pv_done, 4 * GROUPS)
            act.wait_ge(m_ready, m_end)
            act.activation(ot[:, HI, :], M[:, END_BANK, :], ACT.Copy).then_inc(ot_hi, 1)

        @block.vector
        def _(dve):
            def lows(tile):
                g, hh, i = tile
                n = (i + 1) * P
                wait_apart(dve, s_ready, tile_of(g, hh, i) + 1, passed_dve)
                dve.tensor_tensor_reduce(scores_of(i, n), scores_of(i, n), mask[:, N - n:N], 1.0, 3.0e38,
                                         ALU.add, ALU.min, low[:, i % 4:i % 4 + 1]).then_inc(low_ready, 1)

            def inverse(tile):
                g, hh, i = tile
                dve.wait_ge(exp_done, tile_of(g, hh, i) + 1)
                dve.reciprocal(inv[:, i % 4:i % 4 + 1], total[:, i % 4:i % 4 + 1]).then_inc(inv_ready, 1)

            def rest_transposed(g, hh, i):
                for c, (kt0, n) in enumerate(batches(i)):
                    dve.wait_ge(pt_hi, batch_of(g, hh, i) + c + 1)
                    dve.tensor_tensor(pt_cells(LO, i // QT, kt0, n, i % QT), TR[:, (BATCH[i] + c) % 2, 0:n, :],
                                      pt_cells(HI, i // QT, kt0, n, i % QT).bitcast(F32), ALU.subtract)\
                       .then_inc(pt_lo, 1)

            def project_add(m, bank, G, c):
                dve.wait_ge(m_ready, m + 1)
                at = x[:, QT * G + 2 * c:QT * G + 2 * c + 2, :].rearrange("p t d -> p (t d)")
                dve.tensor_tensor(at, M[:, bank, :], at, ALU.add).then_inc(m_read, 1)

            def task(t, g, par, m, n_hi, bank):
                proj = M[:, bank, :] if bank is not None else None
                if t[0] == "S":
                    _, is_k, half = t
                    dve.wait_ge(m_hi, n_hi + 1)
                    for hh in range(2):
                        rows, cols = slice(hh * DS, (hh + 1) * DS), slice(half * HALF, (half + 1) * HALF)
                        hi = qk[rows, par, is_k, hh, HI, cols].bitcast(F32)
                        lo = qk[rows, par, is_k, hh, LO, cols]
                        if is_k:
                            op = dve.tensor_tensor(lo, proj[rows, :], hi, ALU.subtract)
                        else:
                            op = dve.scalar_tensor_tensor(lo, proj[rows, :], s_sem[rows, bass.ds(g, 1)], hi,
                                                          ALU.mult, ALU.subtract)
                    op.then_inc(m_read, 1)
                if t[0] == "G":
                    r = 2 * g + t[1]
                    for which in range(2):
                        dve.wait_ge(geo_hi, 2 * r + which + 1)
                        dve.tensor_tensor(rot[:, 2 * which, :], rot[:, 2 * which, :], rot[:, 2 * which + 1, :],
                                          ALU.subtract).then_inc(geo_lo, 1)
                if t[0] == "V":
                    c = t[1]
                    dve.wait_ge(m_hi, n_hi + 1)
                    dve.tensor_tensor(v[:, LO, 2 * c:2 * c + 2, :].rearrange("p t n -> p (t n)"), proj,
                                      v[:, HI, 2 * c:2 * c + 2, :].rearrange("p t n -> p (t n)").bitcast(F32),
                                      ALU.subtract).then_inc(m_read, 1)
                if t[0] == "PV":
                    dve.wait_ge(ot_hi, 4 * g + t[1] + 1)
                    dve.tensor_tensor(ot[:, LO, :], proj, ot[:, HI, :].bitcast(F32), ALU.subtract)\
                       .then_inc(m_read, 1)
                if t[0] == "W":
                    project_add(m, bank, t[1] % 2, t[2])

            norm.vector(dve)
            dve.memset(s_geo[2 * HALF_G:P, :], 1.0)
            dve.wait_ge(gate_sig, 2)
            dve.tensor_scalar(s_geo[0:2 * HALF_G, :], s_geo[0:2 * HALF_G, :], DG ** -0.5, -DG ** -0.5,
                              ALU.mult, ALU.add)
            dve.tensor_scalar(s_sem[:], s_sem[:], -DS ** -0.5, None, ALU.mult).then_inc(gate_ready, 1)
            dve.wait_ge(gate_ready, 1)
            for t in PRO:
                m = PRO_CHUNKS.index(t) if t in PRO_CHUNKS else None
                n_hi = [s for s in PRO if s[0] == "S"].index(t) if t[0] == "S" else None
                if t[0] != "X":
                    task(t, 0, 0, m, n_hi, m % 2 if m is not None else None)
            dve.wait_ge(mask_ready, 1)
            for i in range(2):
                lows((0, 0, i))
                inverse((0, 0, i))

            def group(g, par, first, last):
                def beside(tasks):
                    for t in tasks:
                        if absent(t, first, last) or t[0] == "X":
                            continue
                        nxt = t[0] in "SG"
                        m = chunk_index(g, t, first, last) if t[0] == "W" else None
                        n_hi = split_index(g, t, first, last) if t[0] in ("V", "S") else None
                        bank = None if t[0] == "G" else bank_of(t, first, last)
                        task(t, g + 1 if nxt else g, 1 - par if nxt else par, m, n_hi, bank)

                for hh in range(2):
                    for i in range(NT):
                        tile = ahead(hh, i, g, last)
                        if tile is not None:
                            lows(tile)
                        beside(BESIDE[hh, i][0])
                        rest_transposed(g, hh, i)
                        if tile is not None:
                            inverse(tile)
                        beside(BESIDE[hh, i][1])

            group(0, 0, True, False)
            with dve.Fori(0, (GROUPS - 2) // 2) as j:
                group(2 * j + 1, 1, False, False)
                group(2 * j + 2, 0, False, False)
            group(GROUPS - 1, 1, False, True)
            m_end = chunk_index(GROUPS - 1, ("W", 2, 1), False, True) + 1
            dve.wait_ge(ot_hi, 4 * GROUPS)
            dve.tensor_tensor(ot[:, LO, :], M[:, END_BANK, :], ot[:, HI, :].bitcast(F32), ALU.subtract)\
               .then_inc(m_read, 1)
            for c in range(2):
                project_add(m_end + c, (END_BANK + 1 + c) % 2, 1, c)

        @block.tensor
        def _(pe):
            def three(out, left, right, start, stop):
                pe.matmul(out, left[0], right[0], start=start, stop=False)
                pe.matmul(out, left[0], right[1], start=False, stop=False)
                return pe.matmul(out, left[1], right[0], start=False, stop=stop)

            def scores(tile, par, qk_done):
                g, hh, i = tile
                T = tile_of(g, hh, i)
                if qk_done is not None:
                    pe.wait_ge(m_read, qk_done)
                    pe.wait_ge(geo_moved, MOVES * 2 * (g + 1))
                back = {0: 1, 1: 2, 2: 2, 3: 3, 4: 2, 5: 1, 6: 1, 7: 1}[i]
                if not isinstance(T, int) or T >= back + (i < 4) * 4:
                    pe.wait_ge(exp_done, T - back)
                q = [qk[:, par, 0, hh, part, i * P:(i + 1) * P] for part in (HI, LO)]
                for c in range(i // QT + 1):
                    n = min(QT, i + 1 - QT * c) * P
                    n = max(n, 2 * P)
                    at = c * HALF
                    keys = [qk[:, par, 1, hh, part, at:at + n] for part in (HI, LO)]
                    bank = S[:, i if i < 4 else 2 * (i % 2) + c, 0:n]
                    last = three(bank, q, keys, True, True)
                last.then_inc(s_ready, 1)

            def transposes(g, hh, i):
                pe.wait_ge(probs_ready, tile_of(g, hh, i) + 1)
                row = probs_of(i, (i + 1) * P)
                for c, (kt0, n) in enumerate(batches(i)):
                    b = batch_of(g, hh, i) + c
                    if not isinstance(b, int) or b >= 2:
                        pe.wait_ge(pt_lo, b - 1)
                    for k in range(n):
                        last = pe.transpose(TR[:, (BATCH[i] + c) % 2, k, :], row[:, (kt0 + k) * P:(kt0 + k + 1) * P],
                                            ident[:])
                    last.then_inc(tr_ready, 1)

            def bank_free(reader):
                is_x, n = reader
                pe.wait_ge(x_read if is_x else m_read, n + 1)

            def values_product(bank, hh, G, batches_done, reader):
                pe.wait_ge(pt_lo, batches_done)
                bank_free(reader)
                kts = QT * (G + 1)
                for kt in range(kts):
                    start = max(0, min(kt - QT * G, 2)) * P
                    at = pt_col(G, kt, 0) + start
                    cells = [pt[:, part, at:at + HALF - start] for part in (HI, LO)]
                    vals = [v[:, part, kt, hh * DV:(hh + 1) * DV] for part in (HI, LO)]
                    last = three(M[:, bank, start:HALF], vals, cells, kt == 0, kt == kts - 1)
                last.then_inc(pv_done, 1)

            def project_out(hh, c, pv_read, bank, reader):
                if c == 0:
                    pe.wait_ge(m_read, pv_read)
                bank_free(reader)
                for j in range(2):
                    cols = slice((2 * c + j) * P, (2 * c + j + 1) * P)
                    last = three(M[:, bank, j * D:(j + 1) * D], [ot[:, part, cols] for part in (HI, LO)],
                                 [wo[:, part, hh * D:(hh + 1) * D] for part in (HI, LO)], True, True)
                last.then_inc(m_ready, 1)

            def project_in(column, half, bank, reader):
                if reader is not None:
                    bank_free(reader)
                for k in range(KD):
                    w = [wqk[:, part, k * QK_COLS + column * P:k * QK_COLS + (column + 1) * P] for part in (HI, LO)]
                    tokens = [xs[:, k, half * HALF:(half + 1) * HALF] for xs in (xh, xl)]
                    last = three(M[:, bank, :], w, tokens, k == 0, k == KD - 1)
                last.then_inc(m_ready, 1)

            def project_values(c, bank, reader):
                bank_free(reader)
                for j in range(2):
                    t = 2 * c + j
                    for k in range(KD):
                        last = three(M[:, bank, j * 2 * DV:(j + 1) * 2 * DV], [xs[:, k, t * P:(t + 1) * P] for xs in (xh, xl)],
                                     [wv[:, part, k * 2 * DV:(k + 1) * 2 * DV] for part in (HI, LO)],
                                     k == 0, k == KD - 1)
                last.then_inc(m_ready, 1)

            norm.tensor(pe)
            pe.wait_ge(pt_zero, 4)
            pe.wait_ge(norm.xlo_ready, 4)
            pe.wait_ge(wqk_lo, 1)
            for t in PRO_CHUNKS:
                m = PRO_CHUNKS.index(t)
                reader = None
                if m >= 2:
                    old = PRO_CHUNKS[m - 2]
                    reader = old[0] == "X", len([p for p in PRO_CHUNKS[:m - 2] if (p[0] == "X") == (old[0] == "X")])
                project_in(2 + t[2] if t[0] == "X" else t[1], t[1] if t[0] == "X" else t[2], m % 2, reader)
            for i in range(2):
                scores((0, 0, i), 0, len([t for t in PRO_CHUNKS if t[0] == "S"]) if i == 0 else None)

            def group(g, par, first, last):
                def beside(tasks):
                    for t in tasks:
                        if absent(t, first, last) or t[0] == "G":
                            continue
                        bank, reader = bank_of(t, first, last), bank_reader(g, t, first, last)
                        if t[0] == "PV":
                            k = t[1] % 4
                            done = 2 * BATCHES * (g - (t[1] < 0)) + BATCHES * (k // 2) + (4 if k % 2 == 0 else 12)
                            if t[1] == 0:
                                pe.wait_ge(m_read, read_index(g, ("V", 3), first, last) + 1)
                            values_product(bank, k // 2, k % 2, done, reader)
                        if t[0] == "X":
                            if t == ("X", 0, 0):
                                pe.wait_ge(wqk_lo, g + 2)
                            project_in(2 + t[2], t[1], bank, reader)
                        if t[0] == "S":
                            project_in(t[1], t[2], bank, reader)
                        if t[0] == "V":
                            if t[1] == 0:
                                pe.wait_ge(wv_lo, g + 1)
                            project_values(t[1], bank, reader)
                        if t[0] == "W":
                            if t[1] == 0:
                                pe.wait_ge(wo_lo, g + 1)
                            project_out((t[1] % 4) // 2, t[2], read_index(g, ("PV", t[1]), first, last) + 1, bank, reader)

                for hh in range(2):
                    for i in range(NT):
                        tile = ahead(hh, i, g, last)
                        if tile is not None:
                            crosses = hh == 1 and i + 2 >= NT
                            done = read_index(g, ("S", 1, 1), first, last) + 1 if crosses and i + 2 == NT else None
                            scores(tile, 1 - par if crosses else par, done)
                        beside(BESIDE[hh, i][0])
                        transposes(g, hh, i)
                        beside(BESIDE[hh, i][1])

            group(0, 0, True, False)
            with pe.Fori(0, (GROUPS - 2) // 2) as j:
                group(2 * j + 1, 1, False, False)
                group(2 * j + 2, 0, False, False)
            group(GROUPS - 1, 1, False, True)
            n = read_index(GROUPS - 1, ("W", 2, 1), False, True)
            values_product(END_BANK, 1, 1, 2 * BATCHES * GROUPS, (False, n - 1))
            for c in range(2):
                project_out(1, c, n + 2, (END_BANK + 1 + c) % 2, (False, n + c))


def build(nc, t):
    with ExitStack() as ctx:
        g = Names(nc, ctx, "all")
        x = g.sb("x", [P, NT, D])
        consts = g.sb("consts", [P, P + NE])
        consts_loaded = g.sem("consts_loaded")
        with nc.Block() as block:
            @block.sync
            def _(sp):
                sp.dma_start(consts[:], t["consts"]).then_inc(consts_loaded, 16)
                sp.wait_ge(consts_loaded, 16)
        comb_dram = nc.dram_tensor("comb_dram", (NE, N), F32, kind="Internal").ap()
        ffn = t["w_ffn"], t["w_router"], t["bias"], comb_dram
        ffn_phase(nc, "f1", x, consts, *ffn, t["x"], None)
        attention_phase(nc, "at", x, consts, t["w_qk"], t["w_v"], t["w_o"], t["gate"], t["rope"])
        ffn_phase(nc, "f2", x, consts, *ffn, None, t["out"])


def layouts(a):
    experts = []
    for j in range(NSH):
        cols = slice(j * F, (j + 1) * F)
        experts.append((a["L0_ffn_Su"][0][:, cols], a["L0_ffn_Sg"][0][:, cols], a["L0_ffn_Sd"][0][cols, :]))
    experts += [(a["L0_ffn_Wu"][e], a["L0_ffn_Wg"][e], a["L0_ffn_Wd"][e]) for e in range(NE)]

    def by_feature(w):
        return w.reshape(KD, P, -1).transpose(1, 0, 2).reshape(P, -1)

    w_ffn = np.stack([np.concatenate([by_feature(u), by_feature(g), d], axis=1) for u, g, d in experts])
    consts = np.concatenate([np.eye(P), np.tile(np.arange(NE), (P, 1))], axis=1).astype(np.float32)

    q_sem, k_sem = (a[f"L0_attn_w{n}_sem"].reshape(D, GROUPS, 2 * DS) for n in "qk")
    geo = np.stack([a[f"L0_attn_w{n}_geo"].reshape(D, GROUPS, 2, 2, HALF_G) for n in "qk"], axis=2)
    x1, x2 = (geo[:, :, :, :, j].reshape(D, GROUPS, P) for j in range(2))
    cols = np.concatenate([q_sem, k_sem, x1, x2], axis=2)
    w_qk = np.stack([by_feature(cols[:, g]) for g in range(GROUPS)])
    w_qk = np.concatenate([w_qk, w_qk[:1]])
    w_v = np.stack([by_feature(a["L0_attn_wv"][:, g * 2 * DV:(g + 1) * 2 * DV]) for g in range(GROUPS)])
    w_o = a["L0_attn_wo"].reshape(GROUPS, 2, DV, D).transpose(0, 2, 1, 3).reshape(GROUPS, P, WO)
    inv_freq = (np.float32(1.0) / np.float32(ROPE_BASE) ** (np.arange(HALF_G, dtype=np.float32) / HALF_G))
    angle = np.arange(N, dtype=np.float32)[None, :] * inv_freq.astype(np.float32)[:, None]
    rope = np.stack([np.tile(f(angle.astype(np.float64)), (4, 1)) for f in (np.cos, np.sin)], axis=1)
    return {
        "w_qk": w_qk,
        "w_v": w_v,
        "w_o": w_o,
        "gate": a["L0_attn_gate_logit"].reshape(GROUPS, 2).T,
        "rope": rope.astype(np.float32),
        "x": a["L0_attn_x"].reshape(N, D),
        "w_ffn": w_ffn,
        "w_router": by_feature(a["L0_ffn_router_w"].T),
        "bias": a["L0_ffn_router_bias"],
        "consts": consts,
    }


def kernel(**inputs):
    import concourse.bacc as bacc
    from concourse.bass_utils import run_bass_kernel_spmd

    arrays = {k: np.ascontiguousarray(v) for k, v in layouts({k: np.asarray(v) for k, v in inputs.items()}).items()}
    nc = bacc.Bacc("TRN2", target_bir_lowering=False, num_devices=1)
    aps = {k: nc.dram_tensor(f"in_{k}", v.shape, mybir.dt.from_np(v.dtype), kind="ExternalInput").ap()
           for k, v in arrays.items()}
    out = nc.dram_tensor("out_0", (N, D), F32, kind="ExternalOutput").ap()
    build(nc, {**aps, "out": out})
    r = run_bass_kernel_spmd(nc, [{f"in_{k}": v for k, v in arrays.items()}], core_ids=[0])
    return r.results[0]["out_0"].reshape(1, N, D)
```

```python
from contextlib import ExitStack

import numpy as np

import concourse.bass as bass
from concourse import mybir

ALU = mybir.AluOpType
ACT = mybir.ActivationFunctionType
F32 = mybir.dt.float32
F32R = mybir.dt.float32r
BF16 = mybir.dt.bfloat16
U32 = mybir.dt.uint32
X = mybir.AxisListType.X

P = 128
N, D = 1024, 256
NT, KD = N // P, D // P
HALF = N // 2
LN_EPS = 1e-5

NE, F, TOPK = 16, 128, 2
NSH = 2
NEXP = NSH + NE
RING = 3
TRIPLES = NEXP // RING
WCOLS = 2 * KD * F + D
UNITS = 2 * NEXP

H, DS, DG, DV = 16, 64, 64, 128
HALF_G = DG // 2
GROUPS = H // 2
QT = 4
NEG = 1.0e9
ROPE_BASE = 10000.0
QK_COLS = 4 * P
WQK = KD * QK_COLS
WV = KD * 2 * DV
WO = 2 * D


def wait_apart(engine, sem, value, passed):
    engine.wait_ge(sem, value)
    if not isinstance(value, int):
        engine.sem_inc(passed, 1)


class Names:

    def __init__(self, nc, ctx, prefix):
        self.nc, self.ctx, self.prefix = nc, ctx, prefix

    def sb(self, name, shape, dt=F32):
        return self.ctx.enter_context(self.nc.sbuf_tensor(f"{self.prefix}_{name}", shape, dt))

    def ps(self, name, shape, dt=F32):
        return self.ctx.enter_context(self.nc.psum_tensor(f"{self.prefix}_{name}", shape, dt))

    def sem(self, name):
        return self.ctx.enter_context(self.nc.semaphore(f"{self.prefix}_{name}"))


class Norm:

    def __init__(self, a, x, ident, banks, xn=None):
        self.x, self.ident, self.banks = x, ident, banks
        self.xh = a.sb("xh", [P, KD, N], F32R)
        self.xl = a.sb("xl", [P, KD, N], F32R)
        self.stats = a.sb("stats", [P, NT, 6])
        self.mv = a.sb("mv", [P, NT, 2])
        self.veps = a.sb("veps", [P, NT])
        self.std = a.sb("std", [P, NT])
        self.rstd = a.sb("rstd", [P, NT])
        self.xn = a.sb("xn", [P, NT, D]) if xn is None else xn
        self.stats_done = a.sem("stats_done")
        self.mv_done = a.sem("mv_done")
        self.veps_ready = a.sem("veps_ready")
        self.std_ready = a.sem("std_ready")
        self.rstd_ready = a.sem("rstd_ready")
        self.xn_ready = a.sem("xn_ready")
        self.xt_tile = a.sem("xt_tile")
        self.xhi_ready = a.sem("xhi_ready")
        self.xlo_ready = a.sem("xlo_ready")

    def vector(self, dve, loaded=None, between=None):
        for t in range(NT):
            if loaded is not None and t % 2 == 0:
                dve.wait_ge(loaded[t // 2], 16)
            dve.bn_stats(self.stats[:, t, :], self.x[:, t, :]).then_inc(self.stats_done, 1)
        for t in range(NT):
            dve.wait_ge(self.stats_done, t + 1)
            dve.bn_aggr(self.mv[:, t, :], self.stats[:, t, :]).then_inc(self.mv_done, 1)
        dve.wait_ge(self.mv_done, NT)
        dve.tensor_scalar(self.veps[:], self.mv[:, :, 1], LN_EPS, None, ALU.add).then_inc(self.veps_ready, 1)
        dve.wait_ge(self.std_ready, 1)
        dve.reciprocal(self.rstd[:], self.std[:]).then_inc(self.rstd_ready, 1)
        dve.wait_ge(self.rstd_ready, 1)
        for t in range(NT):
            dve.tensor_scalar(self.xn[:, t, :], self.x[:, t, :], self.mv[:, t, 0:1], self.rstd[:, t:t + 1],
                              ALU.subtract, ALU.mult).then_inc(self.xn_ready, 1)
        for b in range(2 * KD):
            h, k = divmod(b, KD)
            cols = slice(h * HALF, (h + 1) * HALF)
            if b == KD and between is not None:
                between()
            dve.wait_ge(self.xhi_ready, b + 1)
            dve.tensor_tensor(self.xl[:, k, cols], self.banks[b], self.xh[:, k, cols].bitcast(F32),
                              ALU.subtract).then_inc(self.xlo_ready, 1)

    def scalar_first(self, act):
        act.wait_ge(self.veps_ready, 1)
        act.activation(self.std[:], self.veps[:], ACT.Sqrt).then_inc(self.std_ready, 1)

    def scalar(self, act):
        for b in range(2 * KD):
            h, k = divmod(b, KD)
            act.wait_ge(self.xt_tile, 4 * (h + 1))
            act.activation(self.xh[:, k, h * HALF:(h + 1) * HALF], self.banks[b], ACT.Copy)\
               .then_inc(self.xhi_ready, 1)

    def tensor(self, pe):
        for t in range(NT):
            h, j = divmod(t, 4)
            pe.wait_ge(self.xn_ready, t + 1)
            for k in range(KD):
                last = pe.transpose(self.banks[KD * h + k][:, j * P:(j + 1) * P],
                                    self.xn[:, t, k * P:(k + 1) * P], self.ident[:])
            last.then_inc(self.xt_tile, 1)


def ffn_phase(nc, name, x, consts, w_ffn, w_router, bias, comb_dram, x_in, x_out, consts_in=None):
    with ExitStack() as ctx:
        a = Names(nc, ctx, name)
        Y = a.ps("Y", [P, NT, D])
        UG = a.ps("UG", [P, 2, 2, HALF])
        ident, iota = consts[:, 0:P], consts[:, P:P + NE]
        norm = Norm(a, x, ident, [UG[:, b // 2, b % 2, :] for b in range(4)])
        xh, xl = norm.xh, norm.xl

        w_raw = a.sb("w_raw", [P, RING, WCOLS])
        w_hi = a.sb("w_hi", [P, RING, WCOLS], F32R)
        w_lo = a.sb("w_lo", [P, RING, WCOLS], F32R)
        silu = a.sb("silu", [P, 2, HALF])
        hid = a.sb("hid", [P, 2, HALF])
        hid_hi = a.sb("hid_hi", [P, 3, HALF], F32R)
        hid_lo = a.sb("hid_lo", [P, 3, HALF], F32R)
        comb = a.sb("comb", [P, RING, N])

        rw = a.sb("rw", [P, KD * NE])
        rw_hi = a.sb("rw_hi", [P, KD * NE], F32R)
        rw_lo = a.sb("rw_lo", [P, KD * NE], F32R)
        logit_t = a.sb("logit_t", [NE, N])
        bias_b = a.sb("bias_b", [P, NE])
        logit = a.sb("logit", [P, NT, NE])
        biased = a.sb("biased", [P, NT, NE])
        top = a.sb("top", [P, NT])
        prob = a.sb("prob", [P, NT, NE])
        ssum = a.sb("ssum", [P, NT])
        best = a.sb("best", [P, NT, 8])
        best_at = a.sb("best_at", [P, NT, 8], U32)
        at = a.sb("at", [P, NT, TOPK])
        pick = a.sb("pick", [P, TOPK, NT, NE])
        ksum = a.sb("ksum", [P, NT])
        cw = a.sb("cw", [P, NE, NT])
        cw_t = a.sb("cw_t", [P, P])

        x_loaded = [a.sem(f"x_loaded{b}") for b in range(NT // 2)]
        small_loaded = a.sem("small_loaded")
        w_loaded = [a.sem(f"w_loaded{s}") for s in range(RING)]
        passed_pool = a.sem("passed_pool")
        whi_ready = a.sem("whi_ready")
        wlo_ready = a.sem("wlo_ready")
        rw_hi_ready = a.sem("rw_hi_ready")
        rw_ready = a.sem("rw_ready")
        logits_t_ready = a.sem("logits_t_ready")
        logits_copied = a.sem("logits_copied")
        logits_ready = a.sem("logits_ready")
        route = a.sem("route")
        exp_in = a.sem("exp_in")
        exp_ready = a.sem("exp_ready")
        cw_ready = a.sem("cw_ready")
        cwt_ready = a.sem("cwt_ready")
        cwt_copied = a.sem("cwt_copied")
        cw_stored = a.sem("cw_stored")
        comb_loaded = [a.sem(f"comb_loaded{s}") for s in range(RING)]
        ug_ready = a.sem("ug_ready")
        silu_ready = a.sem("silu_ready")
        prod_done = a.sem("prod_done")
        scaled = a.sem("scaled")
        hhi_ready = a.sem("hhi_ready")
        hlo_ready = a.sem("hlo_ready")
        down_done = a.sem("down_done")
        x_updated = a.sem("x_updated")
        stored = a.sem("stored")

        logits = Y[:, 2, 0:NT * NE]
        cw_back = Y[:, NT - 2, 0:P]
        logits_t = Y[0:NE, NT // 2:NT, :].rearrange("e t n -> e (t n)")

        def up(buf, s, k):
            return buf[:, s, k * F:(k + 1) * F]

        def gate(buf, s, k):
            return buf[:, s, (KD + k) * F:(KD + k + 1) * F]

        def down(buf, s):
            return buf[:, s, 2 * KD * F:WCOLS]

        block = ctx.enter_context(nc.Block())

        @block.sync
        def _(sp):
            if x_in is not None:
                in_v = x_in.rearrange("(b t p) d -> b p t d", p=P, t=2)
                for b in range(NT // 2):
                    sp.dma_start(x[:, 2 * b:2 * b + 2, :], in_v[b]).then_inc(x_loaded[b], 16)
            if consts_in is not None:
                sp.dma_start(consts[:], consts_in[0]).then_inc(consts_in[1], 16)
            sp.dma_start(rw[:], w_router).then_inc(small_loaded, 16)
            sp.dma_start(bias_b[:], bias.partition_broadcast(P)).then_inc(small_loaded, 16)
            for e in range(RING):
                sp.dma_start(w_raw[:, e, :], w_ffn[e]).then_inc(w_loaded[e], 16)
            sp.wait_ge(cwt_copied, 1)
            sp.dma_start(comb_dram.rearrange("e (t n) -> (e t) n", t=NT), cw_t[:]).then_inc(cw_stored, 16)
            sp.wait_ge(cw_stored, 16)
            sp.dma_start(comb[:, NSH, :], comb_dram[0].partition_broadcast(P)).then_inc(comb_loaded[NSH], 16)

            def loads(g, s):
                e = RING * g + s
                sp.wait_ge(wlo_ready, e - 2)
                sp.dma_start(w_raw[:, s, :], w_ffn[bass.ds(e, 1)].rearrange("e p n -> p (e n)"))\
                  .then_inc(w_loaded[s], 16)
                if s < NSH:
                    sp.wait_ge(prod_done, 2 * e - 4)
                sp.wait_ge(hlo_ready, 2 * e - 4)
                sp.dma_start(comb[:, s, :], comb_dram[bass.ds(e - NSH, 1)].rearrange("e n -> (e n)")
                             .partition_broadcast(P)).then_inc(comb_loaded[s], 16)

            with sp.Fori(1, TRIPLES) as g:
                for s in range(RING):
                    loads(g, s)
            if x_out is not None:
                out_v = x_out.rearrange("(b t p) d -> b p t d", p=P, t=2)
                for b in range(NT // 2):
                    sp.wait_ge(x_updated, b + 1)
                    sp.dma_start(out_v[b], x[:, 2 * b:2 * b + 2, :]).then_inc(stored, 16)
                sp.wait_ge(stored, 16 * (NT // 2))
            sp.wait_ge(cw_stored, 16)

        @block.gpsimd
        def _(pool):
            pool.wait_ge(rw_hi_ready, 1)
            pool.tensor_tensor(rw_lo[:], rw[:], rw_hi[:].bitcast(F32), ALU.subtract).then_inc(rw_ready, 1)

            def split_weights(g, s):
                e = RING * g + s
                pool.wait_ge(w_loaded[s], 16 * (g + 1))
                if not isinstance(e, int) or e >= RING:
                    wait_apart(pool, down_done, 2 * e - 4, passed_pool)
                pool.tensor_copy(w_hi[:, s, :], w_raw[:, s, :]).then_inc(whi_ready, 1)
                pool.wait_ge(whi_ready, e + 1)
                pool.tensor_tensor(w_lo[:, s, :], w_raw[:, s, :], w_hi[:, s, :].bitcast(F32), ALU.subtract)\
                    .then_inc(wlo_ready, 1)

            for s in range(RING):
                split_weights(0, s)
            with pool.Fori(1, TRIPLES) as g:
                for s in range(RING):
                    split_weights(g, s)

        @block.scalar
        def _(act):
            def expert(g, s, shared):
                for half in range(2):
                    n = 2 * (RING * g + s) + half
                    act.wait_ge(ug_ready, n + 1)
                    act.activation(silu[:, half, :], UG[:, half, 0, :], ACT.Silu).then_inc(silu_ready, 1)
                    if shared:
                        act.wait_ge(prod_done, n + 1)
                    else:
                        act.wait_ge(scaled, n + 1 - 2 * NSH)
                    r = (2 * s + half) % 3
                    if not isinstance(n, int) or n >= 3:
                        act.wait_ge(down_done, n - 2)
                    act.activation(hid_hi[:, r, :], hid[:, half, :], ACT.Copy).then_inc(hhi_ready, 1)

            norm.scalar_first(act)
            act.wait_ge(small_loaded, 32)
            act.activation(rw_hi[:], rw[:], ACT.Copy).then_inc(rw_hi_ready, 1)
            norm.scalar(act)
            for h in range(2):
                act.wait_ge(logits_t_ready, h + 1)
                cols = slice(h * HALF, (h + 1) * HALF)
                act.activation(logit_t[:, cols], logits_t[:, cols], ACT.Copy).then_inc(logits_copied, 1)
            act.wait_ge(exp_in, 1)
            act.activation(prob[:], prob[:], ACT.Exp).then_inc(exp_ready, 1)
            for s in range(RING):
                expert(0, s, s < NSH)
            with act.Fori(1, TRIPLES) as g:
                for s in range(RING):
                    expert(g, s, False)

        @block.vector
        def _(dve):
            norm.vector(dve, None if x_in is None else x_loaded)
            if consts_in is not None:
                dve.wait_ge(consts_in[1], 16)
            dve.wait_ge(small_loaded, 32)

            def product(n, half, scaled_by):
                dve.wait_ge(silu_ready, n + 1)
                dve.tensor_tensor(hid[:, half, :], UG[:, half, 1, :], silu[:, half, :], ALU.mult)\
                   .then_inc(prod_done, 1)
                if scaled_by:
                    g, s = scaled_by
                    dve.wait_ge(prod_done, n + 1)
                    if half == 0:
                        dve.wait_ge(comb_loaded[s], 16 * (g + s // NSH))
                    dve.tensor_tensor(hid[:, half, :], hid[:, half, :],
                                      comb[:, s, half * HALF:(half + 1) * HALF], ALU.mult).then_inc(scaled, 1)

            def rest(n, s, half):
                r = (2 * s + half) % 3
                dve.wait_ge(hhi_ready, n + 1)
                dve.tensor_tensor(hid_lo[:, r, :], hid[:, half, :], hid_hi[:, r, :].bitcast(F32), ALU.subtract)\
                   .then_inc(hlo_ready, 1)

            def expert(g, s, shared):
                for half in range(2):
                    n = 2 * (RING * g + s) + half
                    product(n, half, None if shared else (g, s))
                    rest(n, s, half)

            steps = [0]

            def step(instruction):
                instruction.then_inc(route, 1)
                steps[0] += 1
                dve.wait_ge(route, steps[0])

            def over_experts(v):
                return v.unsqueeze(2).broadcast_to([P, NT, NE])

            dve.wait_ge(logits_ready, 1)
            step(dve.tensor_copy(logit[:], logits.rearrange("p (t e) -> p t e", e=NE)))
            step(dve.tensor_reduce(top[:], logit[:], X, ALU.max))
            dve.tensor_tensor(prob[:], logit[:], over_experts(top[:]), ALU.subtract).then_inc(exp_in, 1)
            step(dve.tensor_tensor(biased[:], logit[:], bias_b[:].unsqueeze(1).broadcast_to([P, NT, NE]), ALU.add))
            for t in range(NT):
                last = dve.max(best[:, t, :], biased[:, t, :])
            step(last)
            for t in range(NT):
                last = dve.max_index(best_at[:, t, :], best[:, t, :], biased[:, t, :])
            step(last)
            step(dve.tensor_copy(at[:], best_at[:, :, 0:TOPK]))
            product(0, 0, None)
            for k in range(TOPK):
                last = dve.tensor_tensor(pick[:, k, :, :], iota.unsqueeze(1).broadcast_to([P, NT, NE]),
                                         over_experts(at[:, :, k]), ALU.is_equal)
            step(last)
            step(dve.tensor_tensor(pick[:, 0, :, :], pick[:, 0, :, :], pick[:, 1, :, :], ALU.add))
            dve.wait_ge(exp_ready, 1)
            step(dve.tensor_reduce(ssum[:], prob[:], X, ALU.add))
            step(dve.reciprocal(ssum[:], ssum[:]))
            step(dve.tensor_tensor(prob[:], prob[:], over_experts(ssum[:]), ALU.mult))
            step(dve.tensor_tensor(prob[:], prob[:], pick[:, 0, :, :], ALU.mult))
            rest(0, 0, 0)
            product(1, 1, None)
            step(dve.tensor_reduce(ksum[:], prob[:], X, ALU.add))
            step(dve.reciprocal(ksum[:], ksum[:]))
            dve.tensor_tensor(cw[:].rearrange("p e t -> p t e"), prob[:], over_experts(ksum[:]), ALU.mult)\
               .then_inc(cw_ready, 1)

            rest(1, 0, 1)
            dve.wait_ge(cwt_ready, 1)
            dve.tensor_copy(cw_t[:], cw_back).then_inc(cwt_copied, 1)
            for s in range(1, RING):
                expert(0, s, s < NSH)
            with dve.Fori(1, TRIPLES) as g:
                for s in range(RING):
                    expert(g, s, False)
            for b in range(NT // 2):
                dve.wait_ge(down_done, UNITS - 1 + b // 2)
                dve.scalar_tensor_tensor(x[:, 2 * b:2 * b + 2, :].rearrange("p t d -> p (t d)"),
                                         Y[:, 2 * b:2 * b + 2, :].rearrange("p t d -> p (t d)"), 0.5,
                                         x[:, 2 * b:2 * b + 2, :].rearrange("p t d -> p (t d)"),
                                         ALU.mult, ALU.add).then_inc(x_updated, 1)

        @block.tensor
        def _(pe):
            if consts_in is not None:
                pe.wait_ge(consts_in[1], 16)
            norm.tensor(pe)
            pe.wait_ge(rw_ready, 1)
            for h in range(2):
                pe.wait_ge(norm.xlo_ready, KD * (h + 1))
                cols = slice(h * HALF, (h + 1) * HALF)
                for k in range(KD):
                    rk = slice(k * NE, (k + 1) * NE)
                    pe.matmul(logits_t[:, cols], rw_hi[:, rk], xh[:, k, cols], start=(k == 0), stop=False)
                    pe.matmul(logits_t[:, cols], rw_lo[:, rk], xh[:, k, cols], start=False, stop=False)
                    last = pe.matmul(logits_t[:, cols], rw_hi[:, rk], xl[:, k, cols], start=False, stop=(k == KD - 1))
                last.then_inc(logits_t_ready, 1)

            def logits_back():
                for t in range(NT):
                    if t % 4 == 0:
                        pe.wait_ge(logits_copied, t // 4 + 1)
                    last = pe.transpose(logits[:, t * NE:(t + 1) * NE], logit_t[:, t * P:(t + 1) * P],
                                        ident[0:NE, 0:NE])
                last.then_inc(logits_ready, 1)

            def up_gate(s, half):
                cols = slice(half * HALF, (half + 1) * HALF)
                for which, part in ((0, up), (1, gate)):
                    out = UG[:, half, which, :]
                    for k in range(KD):
                        pe.matmul(out, part(w_hi, s, k), xh[:, k, cols], start=(k == 0), stop=False)
                        pe.matmul(out, part(w_hi, s, k), xl[:, k, cols], start=False, stop=False)
                        last = pe.matmul(out, part(w_lo, s, k), xh[:, k, cols], start=False, stop=(k == KD - 1))
                last.then_inc(ug_ready, 1)

            def project_down(n, s, half, first, final):
                pe.wait_ge(hlo_ready, n + 1)
                r = (2 * s + half) % 3
                for j in range(4):
                    out, cols = Y[:, 4 * half + j, :], slice(j * P, (j + 1) * P)
                    pe.matmul(out, hid_hi[:, r, cols], down(w_hi, s), start=(first and j % 2 == 0), stop=False,
                              skip_group_check=True)
                    pe.matmul(out, hid_hi[:, r, cols], down(w_lo, s), start=False, stop=False, skip_group_check=True)
                    last = pe.matmul(out, hid_lo[:, r, cols], down(w_hi, s), start=False,
                                     stop=(final and j % 2 == 1), skip_group_check=True)
                last.then_inc(down_done, 1)

            def expert(g, s, first):
                e = RING * g + s
                pe.wait_ge(wlo_ready, e + 1)
                for half in range(2):
                    n = 2 * e + half
                    if first and n == 0:
                        logits_back()
                    if not first or n >= 2:
                        pe.wait_ge(prod_done, n - 1)
                    up_gate(s, half)
                    if first and n == 3:
                        pe.wait_ge(cwt_copied, 1)
                    if not first or n >= 2:
                        project_down(n - 2, (s - 1) % RING, half, first and s == 1, False)
                    if first and n == 2:
                        pe.wait_ge(cw_ready, 1)
                        pe.transpose(cw_back, cw[:].rearrange("p e t -> p (e t)"), ident[:])\
                          .then_inc(cwt_ready, 1)

            for s in range(RING):
                expert(0, s, True)
            with pe.Fori(1, TRIPLES) as g:
                for s in range(RING):
                    expert(g, s, False)
            for half in range(2):
                project_down(UNITS - 2 + half, RING - 1, half, False, True)



DIAG = 3 * P
DIAG_COLS = 3 * DIAG + QT * P
PT_COLS = 2 * DIAG_COLS + QT * QT * P
LO, HI = 0, 1

P_SLOT = [(0, P), (P, 2 * P), (3 * P, 6 * P), (9 * P, 7 * P), (16 * P, 8 * P),
          (3 * P, 6 * P), (9 * P, 7 * P), (16 * P, 8 * P)]
P_COLS = 24 * P
BATCH = [0, 1, 2, 3, 4, 6, 8, 10]
BATCHES = 12

BESIDE = {
    (0, 0): ([], []),
    (0, 1): ([("X", 0, 0), ("PV", -1)], [("X", 0, 1)]),
    (0, 2): ([("V", 0), ("W", -1, 0)], []),
    (0, 3): ([("V", 1), ("W", -1, 1)], []),
    (0, 4): ([("V", 2), ("G", 0)], [("V", 3)]),
    (0, 5): ([("S", 0, 0)], [("PV", 0)]),
    (0, 6): ([("X", 1, 0)], []),
    (0, 7): ([("X", 1, 1), ("W", 0, 0)], [("W", 0, 1), ("S", 0, 1)]),
    (1, 0): ([], []),
    (1, 1): ([("PV", 1)], []),
    (1, 2): ([], [("W", 1, 0)]),
    (1, 3): ([("S", 1, 0)], []),
    (1, 4): ([("S", 1, 1)], []),
    (1, 5): ([("W", 1, 1), ("G", 1)], [("PV", 2)]),
    (1, 6): ([], []),
    (1, 7): ([("W", 2, 0)], [("W", 2, 1)]),
}
ROPE_OPS = {(0, 1): (0, 0, 4), (0, 2): (0, 4, 6), (1, 1): (1, 0, 2), (1, 2): (1, 2, 4), (1, 3): (1, 4, 6)}
STEPS = [(hh, i) for hh in range(2) for i in range(NT)]
SCORES_AT = dict(zip(STEPS, [1, 0, 0, 0, 0, 0, 0, 0,  0, 0, 2, 0, 1, 0, 1, 0]))
LOWS_AT = dict(zip(STEPS, [0, 0, 0, 0, 0, 0, 0, 0,  1, 0, 0, 0, 0, 0, 1, 0]))
EXPS_AT = dict(zip(STEPS, [3, 1, 1, 3, 2, 2, 2, 2,  1, 3, 3, 2, 3, 2, 0, 3]))
INVERSE_AT = dict(zip(STEPS, [3, 1, 3, 3, 2, 2, 3, 2,  1, 2, 3, 2, 3, 2, 1, 2]))
O_SPLIT, W_SPLIT = (0, 3), (1, 4)
PRO = [("X", 0, 0), ("X", 0, 1), ("X", 1, 0), ("X", 1, 1), ("G", 0), ("S", 0, 0), ("S", 1, 0), ("G", 1),
       ("S", 0, 1), ("S", 1, 1)]


def chunks(first, last):
    order = [t for step in sorted(BESIDE) for part in BESIDE[step] for t in part]
    return [t for t in order if t[0] in "XSVW" and not absent(t, first, last)]


def absent(task, first, last):
    return (first and task[0] in ("PV", "W") and task[1] == -1) or (last and task[0] in ("X", "S", "G"))


PRO_CHUNKS = [t for t in PRO if t[0] != "G"]
PRO_READS = [t for t in PRO_CHUNKS if t[0] != "X"]
FULL = len(chunks(False, False))


def group_base(g, first):
    return len(PRO_CHUNKS) if first else FULL * g + len(PRO_CHUNKS) + len(chunks(True, False)) - FULL


def chunk_index(g, task, first, last):
    return group_base(g, first) + chunks(first, last).index(task)


def ring(first, last):
    order = [t for step in sorted(BESIDE) for part in BESIDE[step] for t in part]
    return [t for t in order if t[0] != "G" and not absent(t, first, last)]


RING_FULL = ring(False, False)
RING_BASE = len(PRO_CHUNKS) + len(ring(True, False)) - len(RING_FULL)


def bank_of(task, first, last):
    return ((len(PRO_CHUNKS) if first else RING_BASE) + ring(first, last).index(task)) % 2


def read_index(g, task, first, last):
    kind = task[0] == "X"
    done, mine, full = ([t for t in tasks if (t[0] == "X") == kind]
                        for tasks in (PRO_CHUNKS, ring(first, last), RING_FULL))
    if first:
        return len(done) + mine.index(task)
    before = [t for t in ring(True, False) if (t[0] == "X") == kind]
    return len(full) * g + len(done) + len(before) - len(full) + mine.index(task)


def reads_before(g, first):
    if first:
        return len(PRO_READS)
    full, ahead = ([t for t in tasks if t[0] != "X"] for tasks in (RING_FULL, ring(True, False)))
    return len(full) * g + len(PRO_READS) + len(ahead) - len(full)


def bank_reader(g, task, first, last):
    order = ring(first, last)
    at = order.index(task) - 2
    if at >= 0:
        return order[at][0] == "X", read_index(g, order[at], first, last)
    if first:
        old = PRO_CHUNKS[at]
        kind = old[0] == "X"
        return kind, [t for t in PRO_CHUNKS if (t[0] == "X") == kind].index(old)
    old = RING_FULL[at]
    kind = old[0] == "X"
    mine = [t for t in RING_FULL if (t[0] == "X") == kind]
    first_of_kind = next(t for t in RING_FULL if (t[0] == "X") == kind)
    return kind, read_index(g, first_of_kind, False, False) - (len(mine) - mine.index(old))


def split_index(g, task, first, last):
    mine = [t for t in chunks(first, last) if t[0] in "VS"]
    return 4 + 8 * g + mine.index(task)


def attention_phase(nc, name, x, consts, w_qk, w_v, w_o, gate, rope):
    with ExitStack() as ctx:
        a = Names(nc, ctx, name)
        S = a.ps("S", [P, 4, HALF])
        TR = a.ps("TR", [P, 2, QT, P])
        M = a.ps("M", [P, 2, HALF])
        ident = consts[:, 0:P]

        probs = a.sb("probs", [P, P_COLS])
        norm = Norm(a, x, ident, [S[:, b, :] for b in range(4)], probs[:, 0:NT * D].rearrange("p (t d) -> p t d", t=NT))
        xh, xl = norm.xh, norm.xl
        qk = a.sb("qk", [P, 2, 2, 2, 2, N], F32R)
        v = a.sb("v", [P, 2, NT, 2 * DV], F32R)
        pt = a.sb("pt", [P, 2, PT_COLS], F32R)
        ot = a.sb("ot", [P, 2, HALF], F32R)
        raw_qk = a.sb("raw_qk", [P, WQK])
        raw_vo = a.sb("raw_vo", [P, WV])
        wqk = a.sb("wqk", [P, 2, WQK], F32R)
        wv = a.sb("wv", [P, 2, WV], F32R)
        wo = a.sb("wo", [P, 2, WO], F32R)
        cs = a.sb("cs", [P, 2, N])
        rot = a.sb("rot", [P, 4, HALF])
        x2 = a.sb("x2", [P, HALF])
        x2s = a.sb("x2s", [P, HALF])
        mask = a.sb("mask", [P, N], BF16)
        s_sem = a.sb("s_sem", [P, GROUPS])
        s_geo = a.sb("s_geo", [P, GROUPS])
        low = a.sb("low", [P, 4])
        total = a.sb("total", [P, 4])
        inv = a.sb("inv", [P, 4])

        tables_loaded = a.sem("tables_loaded")
        gate_loaded = a.sem("gate_loaded")
        gate_exp = a.sem("gate_exp")
        gate_step = a.sem("gate_step")
        gate_ready = a.sem("gate_ready")
        passed_pool = a.sem("passed_pool")
        passed_act = a.sem("passed_act")
        passed_dve = a.sem("passed_dve")
        pt_zero = a.sem("pt_zero")
        mask_zero = a.sem("mask_zero")
        mask_ready = a.sem("mask_ready")
        qk_loaded = a.sem("qk_loaded")
        v_loaded = a.sem("v_loaded")
        o_loaded = a.sem("o_loaded")
        wqk_hi = a.sem("wqk_hi")
        wv_hi = a.sem("wv_hi")
        wo_hi = a.sem("wo_hi")
        wqk_lo = a.sem("wqk_lo")
        wv_lo = a.sem("wv_lo")
        wo_lo = a.sem("wo_lo")
        m_ready = a.sem("m_ready")
        x_read = a.sem("x_read")
        m_read = a.sem("m_read")
        m_hi = a.sem("m_hi")
        first_rope_step = a.sem("first_rope_step")
        rope_step = a.sem("rope_step")
        geo_hi = a.sem("geo_hi")
        geo_lo = a.sem("geo_lo")
        geo_moved = [a.sem(f"geo_moved{half}") for half in range(2)]
        s_ready = a.sem("s_ready")
        low_ready = a.sem("low_ready")
        exp_done = a.sem("exp_done")
        inv_ready = a.sem("inv_ready")
        probs_ready = a.sem("probs_ready")
        tr_ready = a.sem("tr_ready")
        pt_hi = a.sem("pt_hi")
        pt_lo = a.sem("pt_lo")
        pv_done = a.sem("pv_done")
        ot_hi = a.sem("ot_hi")

        MOVES = 8 * 16

        def tile_of(g, hh, i):
            return 2 * NT * g + NT * hh + i

        def batch_of(g, hh, i):
            return 2 * BATCHES * g + BATCHES * hh + BATCH[i]

        def probs_of(i, n):
            at, _ = P_SLOT[i]
            return probs[:, at:at + n]

        def scores_of(i, n):
            at = i * HALF if i < 4 else (i % 2) * N
            return S[:].rearrange("p b n -> p (b n)")[:, at:at + n]

        def pt_col(G, kt, qj):
            base = G * DIAG_COLS
            if kt < QT * G:
                return base + kt * QT * P + qj * P
            return base + QT * P * QT * G + (kt - QT * G) * DIAG + qj * P

        def pt_cells(part, G, kt0, n, qj):
            stride = QT * P if kt0 < QT * G else DIAG
            at = pt_col(G, kt0, qj)
            if n == 1:
                return pt[:, part, at:at + P].unsqueeze(1)
            return pt[:, part, at:at + n * stride].rearrange("p (k n) -> p k n", n=stride)[:, :, 0:P] \
                if at + n * stride <= PT_COLS else tail_cells(part, at, n, stride)

        def tail_cells(part, at, n, stride):
            shift = at + n * stride - PT_COLS
            return pt[:, part, at - shift:PT_COLS].rearrange("p (k n) -> p k n", n=stride)[:, :, shift:shift + P]

        def batches(i):
            return [(QT * c, min(QT, i + 1 - QT * c)) for c in range(i // QT + 1)]

        def ahead(hh, i, group, last):
            if i + 2 < NT:
                return group, hh, i + 2
            if hh == 0:
                return group, 1, i + 2 - NT
            return None if last else (group + 1, 0, i + 2 - NT)

        def rope_ops(engine, r, half, start, stop):
            cols = slice(half * HALF, (half + 1) * HALF)
            cos, sin = cs[:, 0, cols], cs[:, 1, cols]
            turned, second, product = rope_buffers(r)
            o1, x1 = turned[:, 0, :], turned[:, 2, :]
            step, done = (first_rope_step, 0) if isinstance(r, int) and r == 0 else (rope_step, 6 * (r - 1))
            for k in range(start, stop):
                if k == 0:
                    engine.wait_ge(x_read, 2 * r + 2)
                    op = engine.tensor_tensor(o1, x1, cos, ALU.mult)
                if k == 1:
                    op = engine.tensor_tensor(product, second, sin, ALU.mult)
                if k == 2:
                    engine.wait_ge(step, done + 2)
                    op = engine.tensor_tensor(o1, o1, product, ALU.subtract)
                if k == 3:
                    op = engine.tensor_tensor(x1, x1, sin, ALU.mult)
                if k == 4:
                    op = engine.tensor_tensor(second, second, cos, ALU.mult)
                if k == 5:
                    engine.wait_ge(step, done + 5)
                    op = engine.tensor_tensor(x1, x1, second, ALU.add)
                op.then_inc(step, 1)

        END_BANK = (bank_of(("W", 2, 1), False, True) + 1) % 2

        x2_b, x2s_b = (probs[:, b * HALF:(b + 1) * HALF] for b in range(2))
        rot_b = probs[:, N:N + 4 * HALF].rearrange("p (b n) -> p b n", n=HALF)

        def rope_buffers(r):
            return (rot_b, x2_b, x2s_b) if isinstance(r, int) and r == 1 else (rot[:], x2[:], x2s[:])

        block = ctx.enter_context(nc.Block())

        @block.sync
        def _(sp):
            def load_qk(g):
                sp.dma_start(raw_qk[:], w_qk[bass.ds(g, 1)].rearrange("g p n -> p (g n)")).then_inc(qk_loaded, 16)

            def load_v(g):
                sp.dma_start(raw_vo[:], w_v[bass.ds(g, 1)].rearrange("g p n -> p (g n)")).then_inc(v_loaded, 16)

            def load_o(g):
                sp.dma_start(raw_vo[:], w_o[bass.ds(g, 1)].rearrange("g p n -> p (g n)")).then_inc(o_loaded, 16)

            def move_geo(g, par, half):
                cols = slice(half * HALF, (half + 1) * HALF)
                turned, _, _ = rope_buffers(2 * g + half)
                for which in range(2):
                    sp.wait_ge(geo_lo, 2 * (2 * g + half) + which + 1)
                    for block_ in range(4):
                        is_k, hh = divmod(block_, 2)
                        to = HALF_G * which + (DS if hh == 0 else 0)
                        sp.dma_start(qk[to:to + HALF_G, par, is_k, hh, :, cols].bitcast(F32),
                                     turned[HALF_G * block_:HALF_G * (block_ + 1), 2 * which:2 * which + 2, :])\
                          .then_inc(geo_moved[half], 16)

            load_qk(0)
            for b in range(2):
                sp.dma_start(s_sem[b * DS:(b + 1) * DS, :], gate[b].partition_broadcast(DS)).then_inc(gate_loaded, 16)
                sp.dma_start(s_geo[b * HALF_G:(b + 1) * HALF_G, :], gate[b].partition_broadcast(HALF_G))\
                  .then_inc(gate_loaded, 16)
            load_v(0)
            sp.dma_start(cs[:], rope).then_inc(tables_loaded, 16)
            sp.wait_ge(wqk_lo, 1)
            load_qk(1)
            sp.wait_ge(wv_lo, 1)
            load_o(0)
            for half in range(2):
                move_geo(0, 0, half)

            def group(g, par, last):
                if not last:
                    sp.wait_ge(wqk_lo, g + 2)
                    load_qk(g + 2)
                    move_geo(g + 1, 1 - par, 0)
                    sp.wait_ge(wo_lo, g + 1)
                    load_v(g + 1)
                    move_geo(g + 1, 1 - par, 1)
                    sp.wait_ge(wv_lo, g + 2)
                    load_o(g + 1)

            group(0, 0, False)
            with sp.Fori(0, (GROUPS - 2) // 2) as i:
                group(2 * i + 1, 1, False)
                group(2 * i + 2, 0, False)
            group(GROUPS - 1, 1, True)

        @block.gpsimd
        def _(pool):
            def split(sem, done, n, lo, raw, hi):
                pool.wait_ge(sem, n)
                pool.tensor_tensor(lo, raw, hi.bitcast(F32), ALU.subtract).then_inc(done, 1)

            def normalize(tile):
                g, hh, i = tile
                T = tile_of(g, hh, i)
                wait_apart(pool, inv_ready, T + 1, passed_pool)
                row = probs_of(i, (i + 1) * P)
                pool.tensor_scalar(row, row, inv[:, i % 4:i % 4 + 1], 1.0, ALU.mult, ALU.mult)\
                    .then_inc(probs_ready, 1)

            pool.memset(mask[:], 0.0).then_inc(mask_zero, 1)
            for part in (LO, HI):
                for G in range(2):
                    at = pt_col(G, QT * G + 3, 2)
                    pool.memset(pt[:, part, at:at + P].bitcast(F32), 0.0).then_inc(pt_zero, 1)
            pool.wait_ge(mask_zero, 1)
            pool.affine_select(out=mask[:, N - P:N], in_=mask[:, N - P:N], compare_op=ALU.is_ge, fill=NEG,
                               base=0, pattern=[[-1, P]], channel_multiplier=1).then_inc(mask_ready, 1)
            split(wqk_hi, wqk_lo, 1, wqk[:, LO, :], raw_qk[:], wqk[:, HI, :])
            split(wv_hi, wv_lo, 1, wv[:, LO, :], raw_vo[:], wv[:, HI, :])
            pool.wait_ge(tables_loaded, 16)
            rope_ops(pool, 1, 1, 0, 6)
            split(wqk_hi, wqk_lo, 2, wqk[:, LO, :], raw_qk[:], wqk[:, HI, :])
            for i in range(2):
                normalize((0, 0, i))

            def group(g, par, first, last):
                for hh in range(2):
                    for i in range(NT):
                        tile = ahead(hh, i, g, last)
                        if tile is not None:
                            normalize(tile)
                        if not last and (hh, i) in ROPE_OPS:
                            half, start, stop = ROPE_OPS[hh, i]
                            rope_ops(pool, 2 * g + 2 + half, half, start, stop)
                        if (hh, i) == O_SPLIT:
                            split(wo_hi, wo_lo, g + 1, wo[:, LO, :], raw_vo[:], wo[:, HI, :])
                        if (hh, i) == W_SPLIT and not last:
                            split(wqk_hi, wqk_lo, g + 3, wqk[:, LO, :], raw_qk[:], wqk[:, HI, :])
                            split(wv_hi, wv_lo, g + 2, wv[:, LO, :], raw_vo[:], wv[:, HI, :])

            group(0, 0, True, False)
            with pool.Fori(0, (GROUPS - 2) // 2) as j:
                group(2 * j + 1, 1, False, False)
                group(2 * j + 2, 0, False, False)
            group(GROUPS - 1, 1, False, True)

        @block.scalar
        def _(act):
            def exps(tile):
                g, hh, i = tile
                T = tile_of(g, hh, i)
                act.wait_ge(low_ready, T + 1)
                if isinstance(T, int) and T == 3:
                    act.wait_ge(geo_moved[1], MOVES)
                if not isinstance(T, int) or T >= 3:
                    j = (i - 3) % NT
                    act.wait_ge(tr_ready, batch_of(g, hh, j) + len(batches(j)) - (BATCHES if i < 3 else 0))
                n = (i + 1) * P
                act.activation(probs_of(i, n), scores_of(i, n), ACT.Exp, bias=low[:, i % 4:i % 4 + 1], scale=-1.0,
                               accum_out=total[:, i % 4:i % 4 + 1]).then_inc(exp_done, 1)

            def round_transposed(g, hh, i):
                for c, (kt0, n) in enumerate(batches(i)):
                    b = batch_of(g, hh, i) + c
                    act.wait_ge(tr_ready, b + 1)
                    if c == 0 and i % QT == 0 and (not isinstance(g, int) or 4 * g + 2 * hh + i // QT >= 2):
                        act.wait_ge(pv_done, 4 * g + 2 * hh + i // QT - 1)
                    act.activation(pt_cells(HI, i // QT, kt0, n, i % QT), TR[:, (BATCH[i] + c) % 2, 0:n, :], ACT.Copy)\
                       .then_inc(pt_hi, 1)

            def task(t, g, par, first, last, m, bank):
                proj = M[:, bank, :] if bank is not None else None
                if t[0] == "X":
                    _, half, which = t
                    if isinstance(g, int) and g == 1 and half == 0:
                        act.wait_ge(geo_moved[0], MOVES)
                    elif not isinstance(g, int) or g > 0:
                        act.wait_ge(geo_moved[1 - half], MOVES * (g + half))
                    wait_apart(act, m_ready, m + 1, passed_act)
                    turned, second, _ = rope_buffers(2 * g + half)
                    act.activation(turned[:, 2, :] if which == 0 else second, proj, ACT.Copy,
                                   scale=s_geo[:, bass.ds(g, 1)]).then_inc(x_read, 1)
                if t[0] == "S":
                    _, is_k, half = t
                    wait_apart(act, m_ready, m + 1, passed_act)
                    for hh in range(2):
                        rows = slice(hh * DS, (hh + 1) * DS)
                        out = qk[rows, par, is_k, hh, HI, half * HALF:(half + 1) * HALF]
                        if is_k:
                            op = act.activation(out, proj[rows, :], ACT.Copy)
                        else:
                            op = act.activation(out, proj[rows, :], ACT.Copy, scale=s_sem[rows, bass.ds(g, 1)])
                    op.then_inc(m_hi, 1)
                if t[0] == "G":
                    r = 2 * g + t[1]
                    turned, _, _ = rope_buffers(r)
                    for which in range(2):
                        if isinstance(r, int) and r == 0:
                            act.wait_ge(first_rope_step, 3 * (which + 1))
                        else:
                            act.wait_ge(rope_step, 6 * (r - 1) + 3 * (which + 1))
                        act.activation(turned[:, 2 * which + 1, :].bitcast(F32R), turned[:, 2 * which, :], ACT.Copy)\
                           .then_inc(geo_hi, 1)
                if t[0] == "V":
                    c = t[1]
                    act.wait_ge(m_ready, m + 1)
                    if c == 0 and not first:
                        act.wait_ge(pv_done, 4 * g)
                    act.activation(v[:, HI, 2 * c:2 * c + 2, :].rearrange("p t n -> p (t n)"), proj, ACT.Copy)\
                       .then_inc(m_hi, 1)
                if t[0] == "PV":
                    u = 4 * g + t[1]
                    act.wait_ge(pv_done, u + 1)
                    if not (first and t[1] == 0):
                        act.wait_ge(m_ready, m)
                    act.activation(ot[:, HI, :], proj, ACT.Copy).then_inc(ot_hi, 1)

            def split(sem, n, done, hi, raw, after=None):
                act.wait_ge(sem, 16 * n)
                if after is not None:
                    act.wait_ge(m_ready, after)
                act.activation(hi, raw, ACT.Copy).then_inc(done, 1)

            norm.scalar_first(act)
            split(qk_loaded, 1, wqk_hi, wqk[:, HI, :], raw_qk[:])
            act.wait_ge(gate_loaded, 64)
            act.activation(s_sem[:], s_sem[:], ACT.Exp, scale=-1.0).then_inc(gate_exp, 1)
            act.activation(s_geo[0:2 * HALF_G, :], s_geo[0:2 * HALF_G, :], ACT.Exp, scale=-1.0).then_inc(gate_exp, 1)
            norm.scalar(act)
            split(v_loaded, 1, wv_hi, wv[:, HI, :], raw_vo[:])
            act.wait_ge(gate_ready, 1)
            for t in PRO:
                m = PRO_CHUNKS.index(t) if t in PRO_CHUNKS else None
                if t == ("S", 1, 1):
                    split(qk_loaded, 2, wqk_hi, wqk[:, HI, :], raw_qk[:], len(PRO_CHUNKS))
                task(t, 0, 0, True, False, m, m % 2 if m is not None else None)
            for i in range(2):
                exps((0, 0, i))

            def group(g, par, first, last):
                def beside(tasks):
                    for t in tasks:
                        if absent(t, first, last):
                            continue
                        nxt = t[0] in "XSG"
                        if t[0] in ("X", "S", "V"):
                            m = chunk_index(g, t, first, last)
                        elif t[0] == "PV" and not (first and t[1] == 0):
                            m = chunk_index(g, ("W", t[1] - 1, 1), first, last) + 1 if t[1] >= 0 else \
                                group_base(g, first)
                        else:
                            m = None
                        bank = None if t[0] == "G" else bank_of(t, first, last)
                        task(t, g + 1 if nxt else g, 1 - par if nxt else par, first, last, m, bank)

                for hh in range(2):
                    for i in range(NT):
                        tile = ahead(hh, i, g, last)
                        for part in range(4):
                            if tile is not None and EXPS_AT[hh, i] == part:
                                exps(tile)
                            if part == 1:
                                round_transposed(g, hh, i)
                            elif part < 3:
                                beside(BESIDE[hh, i][part // 2])
                        if (hh, i) == O_SPLIT:
                            after = None if first else chunk_index(g, ("W", -1, 1), first, last) + 1
                            split(o_loaded, g + 1, wo_hi, wo[:, HI, :], raw_vo[:], after)
                        if (hh, i) == W_SPLIT and not last:
                            split(qk_loaded, g + 3, wqk_hi, wqk[:, HI, :], raw_qk[:],
                                  chunk_index(g, ("S", 1, 1), first, last) + 1)
                            split(v_loaded, g + 2, wv_hi, wv[:, HI, :], raw_vo[:])

            group(0, 0, True, False)
            with act.Fori(0, (GROUPS - 2) // 2) as j:
                group(2 * j + 1, 1, False, False)
                group(2 * j + 2, 0, False, False)
            group(GROUPS - 1, 1, False, True)
            m_end = chunk_index(GROUPS - 1, ("W", 2, 1), False, True) + 1
            act.wait_ge(pv_done, 4 * GROUPS)
            act.wait_ge(m_ready, m_end)
            act.activation(ot[:, HI, :], M[:, END_BANK, :], ACT.Copy).then_inc(ot_hi, 1)

        @block.vector
        def _(dve):
            def lows(tile):
                g, hh, i = tile
                n = (i + 1) * P
                wait_apart(dve, s_ready, tile_of(g, hh, i) + 1, passed_dve)
                dve.tensor_tensor_reduce(scores_of(i, n), scores_of(i, n), mask[:, N - n:N], 1.0, 3.0e38,
                                         ALU.add, ALU.min, low[:, i % 4:i % 4 + 1]).then_inc(low_ready, 1)

            def inverse(tile):
                g, hh, i = tile
                dve.wait_ge(exp_done, tile_of(g, hh, i) + 1)
                dve.reciprocal(inv[:, i % 4:i % 4 + 1], total[:, i % 4:i % 4 + 1]).then_inc(inv_ready, 1)

            def rest_transposed(g, hh, i):
                for c, (kt0, n) in enumerate(batches(i)):
                    dve.wait_ge(pt_hi, batch_of(g, hh, i) + c + 1)
                    dve.tensor_tensor(pt_cells(LO, i // QT, kt0, n, i % QT), TR[:, (BATCH[i] + c) % 2, 0:n, :],
                                      pt_cells(HI, i // QT, kt0, n, i % QT).bitcast(F32), ALU.subtract)\
                       .then_inc(pt_lo, 1)

            def project_add(m, bank, G, c):
                dve.wait_ge(m_ready, m + 1)
                at = x[:, QT * G + 2 * c:QT * G + 2 * c + 2, :].rearrange("p t d -> p (t d)")
                dve.tensor_tensor(at, M[:, bank, :], at, ALU.add).then_inc(m_read, 1)

            def task(t, g, par, m, n_hi, bank):
                proj = M[:, bank, :] if bank is not None else None
                if t[0] == "S":
                    _, is_k, half = t
                    dve.wait_ge(m_hi, n_hi + 1)
                    for hh in range(2):
                        rows, cols = slice(hh * DS, (hh + 1) * DS), slice(half * HALF, (half + 1) * HALF)
                        hi = qk[rows, par, is_k, hh, HI, cols].bitcast(F32)
                        lo = qk[rows, par, is_k, hh, LO, cols]
                        if is_k:
                            op = dve.tensor_tensor(lo, proj[rows, :], hi, ALU.subtract)
                        else:
                            op = dve.scalar_tensor_tensor(lo, proj[rows, :], s_sem[rows, bass.ds(g, 1)], hi,
                                                          ALU.mult, ALU.subtract)
                    op.then_inc(m_read, 1)
                if t[0] == "G":
                    r = 2 * g + t[1]
                    turned, _, _ = rope_buffers(r)
                    for which in range(2):
                        dve.wait_ge(geo_hi, 2 * r + which + 1)
                        dve.tensor_tensor(turned[:, 2 * which, :], turned[:, 2 * which, :], turned[:, 2 * which + 1, :],
                                          ALU.subtract).then_inc(geo_lo, 1)
                if t[0] == "V":
                    c = t[1]
                    dve.wait_ge(m_hi, n_hi + 1)
                    dve.tensor_tensor(v[:, LO, 2 * c:2 * c + 2, :].rearrange("p t n -> p (t n)"), proj,
                                      v[:, HI, 2 * c:2 * c + 2, :].rearrange("p t n -> p (t n)").bitcast(F32),
                                      ALU.subtract).then_inc(m_read, 1)
                if t[0] == "PV":
                    dve.wait_ge(ot_hi, 4 * g + t[1] + 1)
                    dve.tensor_tensor(ot[:, LO, :], proj, ot[:, HI, :].bitcast(F32), ALU.subtract)\
                       .then_inc(m_read, 1)
                if t[0] == "W":
                    project_add(m, bank, t[1] % 2, t[2])

            def gates_ready():
                dve.memset(s_geo[2 * HALF_G:P, :], 1.0)
                dve.wait_ge(gate_exp, 2)
                gates = (s_sem[:], s_geo[0:2 * HALF_G, :])
                for s in gates:
                    dve.tensor_scalar(s, s, 1.0, None, ALU.add).then_inc(gate_step, 1)
                for n, s in enumerate(gates):
                    dve.wait_ge(gate_step, n + 1)
                    dve.reciprocal(s, s).then_inc(gate_step, 1)
                dve.wait_ge(gate_step, 4)
                dve.tensor_scalar(s_geo[0:2 * HALF_G, :], s_geo[0:2 * HALF_G, :], DG ** -0.5, -DG ** -0.5,
                                  ALU.mult, ALU.add)
                dve.tensor_scalar(s_sem[:], s_sem[:], -DS ** -0.5, None, ALU.mult).then_inc(gate_ready, 1)

            norm.vector(dve, None, gates_ready)
            dve.wait_ge(gate_ready, 1)
            for t in PRO:
                m = PRO_CHUNKS.index(t) if t in PRO_CHUNKS else None
                n_hi = [s for s in PRO if s[0] == "S"].index(t) if t[0] == "S" else None
                if t == ("G", 0):
                    dve.wait_ge(tables_loaded, 16)
                    rope_ops(dve, 0, 0, 0, 6)
                if t == ("S", 1, 1):
                    dve.wait_ge(mask_ready, 1)
                    for i in range(2):
                        lows((0, 0, i))
                if t[0] != "X":
                    task(t, 0, 0, m, n_hi, m % 2 if m is not None else None)
            for i in range(2):
                inverse((0, 0, i))

            def group(g, par, first, last):
                def beside(tasks):
                    for t in tasks:
                        if absent(t, first, last) or t[0] == "X":
                            continue
                        nxt = t[0] in "SG"
                        m = chunk_index(g, t, first, last) if t[0] == "W" else None
                        n_hi = split_index(g, t, first, last) if t[0] in ("V", "S") else None
                        bank = None if t[0] == "G" else bank_of(t, first, last)
                        task(t, g + 1 if nxt else g, 1 - par if nxt else par, m, n_hi, bank)

                for hh in range(2):
                    for i in range(NT):
                        tile = ahead(hh, i, g, last)
                        for part in range(4):
                            if tile is not None and LOWS_AT[hh, i] == part:
                                lows(tile)
                            if tile is not None and INVERSE_AT[hh, i] == part:
                                inverse(tile)
                            if part == 1:
                                rest_transposed(g, hh, i)
                            elif part < 3:
                                beside(BESIDE[hh, i][part // 2])

            group(0, 0, True, False)
            with dve.Fori(0, (GROUPS - 2) // 2) as j:
                group(2 * j + 1, 1, False, False)
                group(2 * j + 2, 0, False, False)
            group(GROUPS - 1, 1, False, True)
            m_end = chunk_index(GROUPS - 1, ("W", 2, 1), False, True) + 1
            dve.wait_ge(ot_hi, 4 * GROUPS)
            dve.tensor_tensor(ot[:, LO, :], M[:, END_BANK, :], ot[:, HI, :].bitcast(F32), ALU.subtract)\
               .then_inc(m_read, 1)
            for c in range(2):
                project_add(m_end + c, (END_BANK + 1 + c) % 2, 1, c)

        @block.tensor
        def _(pe):
            def three(out, left, right, start, stop):
                pe.matmul(out, left[0], right[0], start=start, stop=False)
                pe.matmul(out, left[0], right[1], start=False, stop=False)
                return pe.matmul(out, left[1], right[0], start=False, stop=stop)

            def scores(tile, par, qk_done):
                g, hh, i = tile
                T = tile_of(g, hh, i)
                if qk_done is not None:
                    pe.wait_ge(m_read, qk_done)
                    pe.wait_ge(geo_moved[i // QT], MOVES * (g + 1))
                back = {0: 1, 1: 2, 2: 2, 3: 3, 4: 2, 5: 1, 6: 1, 7: 1}[i]
                if not isinstance(T, int) or T >= back + (i < 4) * 4:
                    pe.wait_ge(exp_done, T - back)
                q = [qk[:, par, 0, hh, part, i * P:(i + 1) * P] for part in (HI, LO)]
                for c in range(i // QT + 1):
                    n = min(QT, i + 1 - QT * c) * P
                    n = max(n, 2 * P)
                    at = c * HALF
                    keys = [qk[:, par, 1, hh, part, at:at + n] for part in (HI, LO)]
                    bank = S[:, i if i < 4 else 2 * (i % 2) + c, 0:n]
                    last = three(bank, q, keys, True, True)
                last.then_inc(s_ready, 1)

            def transposes(g, hh, i):
                pe.wait_ge(probs_ready, tile_of(g, hh, i) + 1)
                row = probs_of(i, (i + 1) * P)
                for c, (kt0, n) in enumerate(batches(i)):
                    b = batch_of(g, hh, i) + c
                    if not isinstance(b, int) or b >= 2:
                        pe.wait_ge(pt_lo, b - 1)
                    for k in range(n):
                        last = pe.transpose(TR[:, (BATCH[i] + c) % 2, k, :], row[:, (kt0 + k) * P:(kt0 + k + 1) * P],
                                            ident[:])
                    last.then_inc(tr_ready, 1)

            def bank_free(reader):
                is_x, n = reader
                pe.wait_ge(x_read if is_x else m_read, n + 1)

            def values_product(bank, hh, G, batches_done, reader):
                pe.wait_ge(pt_lo, batches_done)
                bank_free(reader)
                kts = QT * (G + 1)
                for kt in range(kts):
                    start = max(0, min(kt - QT * G, 2)) * P
                    at = pt_col(G, kt, 0) + start
                    cells = [pt[:, part, at:at + HALF - start] for part in (HI, LO)]
                    vals = [v[:, part, kt, hh * DV:(hh + 1) * DV] for part in (HI, LO)]
                    last = three(M[:, bank, start:HALF], vals, cells, kt == 0, kt == kts - 1)
                last.then_inc(pv_done, 1)

            def project_out(hh, c, pv_read, bank, reader):
                if c == 0:
                    pe.wait_ge(m_read, pv_read)
                bank_free(reader)
                for j in range(2):
                    cols = slice((2 * c + j) * P, (2 * c + j + 1) * P)
                    last = three(M[:, bank, j * D:(j + 1) * D], [ot[:, part, cols] for part in (HI, LO)],
                                 [wo[:, part, hh * D:(hh + 1) * D] for part in (HI, LO)], True, True)
                last.then_inc(m_ready, 1)

            def project_in(column, half, bank, reader):
                if reader is not None:
                    bank_free(reader)
                for k in range(KD):
                    w = [wqk[:, part, k * QK_COLS + column * P:k * QK_COLS + (column + 1) * P] for part in (HI, LO)]
                    tokens = [xs[:, k, half * HALF:(half + 1) * HALF] for xs in (xh, xl)]
                    last = three(M[:, bank, :], w, tokens, k == 0, k == KD - 1)
                last.then_inc(m_ready, 1)

            def project_values(c, bank, reader):
                bank_free(reader)
                for j in range(2):
                    t = 2 * c + j
                    for k in range(KD):
                        last = three(M[:, bank, j * 2 * DV:(j + 1) * 2 * DV], [xs[:, k, t * P:(t + 1) * P] for xs in (xh, xl)],
                                     [wv[:, part, k * 2 * DV:(k + 1) * 2 * DV] for part in (HI, LO)],
                                     k == 0, k == KD - 1)
                last.then_inc(m_ready, 1)

            norm.tensor(pe)
            pe.wait_ge(pt_zero, 4)
            pe.wait_ge(wqk_lo, 1)
            for t in PRO_CHUNKS:
                m = PRO_CHUNKS.index(t)
                pe.wait_ge(norm.xlo_ready, KD * ((t[1] if t[0] == "X" else t[2]) + 1))
                reader = None
                if m >= 2:
                    old = PRO_CHUNKS[m - 2]
                    reader = old[0] == "X", len([p for p in PRO_CHUNKS[:m - 2] if (p[0] == "X") == (old[0] == "X")])
                project_in(2 + t[2] if t[0] == "X" else t[1], t[1] if t[0] == "X" else t[2], m % 2, reader)
            for i in range(2):
                scores((0, 0, i), 0, PRO_READS.index(("S", 1, 0)) + 1 if i == 0 else None)

            def group(g, par, first, last):
                def beside(tasks):
                    for t in tasks:
                        if absent(t, first, last) or t[0] == "G":
                            continue
                        bank, reader = bank_of(t, first, last), bank_reader(g, t, first, last)
                        if t[0] == "PV":
                            k = t[1] % 4
                            done = 2 * BATCHES * (g - (t[1] < 0)) + BATCHES * (k // 2) + (4 if k % 2 == 0 else 12)
                            if t[1] == 0:
                                pe.wait_ge(m_read, read_index(g, ("V", 3), first, last) + 1)
                            values_product(bank, k // 2, k % 2, done, reader)
                        if t[0] == "X":
                            if t == ("X", 0, 0):
                                pe.wait_ge(wqk_lo, g + 2)
                            project_in(2 + t[2], t[1], bank, reader)
                        if t[0] == "S":
                            project_in(t[1], t[2], bank, reader)
                        if t[0] == "V":
                            if t[1] == 0:
                                pe.wait_ge(wv_lo, g + 1)
                            project_values(t[1], bank, reader)
                        if t[0] == "W":
                            if t[1] == 0:
                                pe.wait_ge(wo_lo, g + 1)
                            project_out((t[1] % 4) // 2, t[2], read_index(g, ("PV", t[1]), first, last) + 1, bank, reader)

                for hh in range(2):
                    for i in range(NT):
                        tile = ahead(hh, i, g, last)
                        for part in range(4):
                            if tile is not None and SCORES_AT[hh, i] == part:
                                crosses = hh == 1 and i + 2 >= NT
                                done = None
                                if crosses and i + 2 == NT:
                                    done = read_index(g, ("S", 1, 0), first, last) + 1
                                if (hh, i + 2) == (0, QT):
                                    done = reads_before(g, first)
                                scores(tile, 1 - par if crosses else par, done)
                            if part == 1:
                                transposes(g, hh, i)
                            elif part < 3:
                                beside(BESIDE[hh, i][part // 2])

            group(0, 0, True, False)
            with pe.Fori(0, (GROUPS - 2) // 2) as j:
                group(2 * j + 1, 1, False, False)
                group(2 * j + 2, 0, False, False)
            group(GROUPS - 1, 1, False, True)
            n = read_index(GROUPS - 1, ("W", 2, 1), False, True)
            values_product(END_BANK, 1, 1, 2 * BATCHES * GROUPS, (False, n - 1))
            for c in range(2):
                project_out(1, c, n + 2, (END_BANK + 1 + c) % 2, (False, n + c))


def build(nc, t):
    with ExitStack() as ctx:
        g = Names(nc, ctx, "all")
        x = g.sb("x", [P, NT, D])
        consts = g.sb("consts", [P, P + NE])
        consts_loaded = g.sem("consts_loaded")
        comb_dram = nc.dram_tensor("comb_dram", (NE, N), F32, kind="Internal").ap()
        ffn = t["w_ffn"], t["w_router"], t["bias"], comb_dram
        ffn_phase(nc, "f1", x, consts, *ffn, t["x"], None, (t["consts"], consts_loaded))
        attention_phase(nc, "at", x, consts, t["w_qk"], t["w_v"], t["w_o"], t["gate"], t["rope"])
        ffn_phase(nc, "f2", x, consts, *ffn, None, t["out"])


def layouts(a):
    experts = []
    for j in range(NSH):
        cols = slice(j * F, (j + 1) * F)
        experts.append((a["L0_ffn_Su"][0][:, cols], a["L0_ffn_Sg"][0][:, cols], a["L0_ffn_Sd"][0][cols, :]))
    experts += [(a["L0_ffn_Wu"][e], a["L0_ffn_Wg"][e], a["L0_ffn_Wd"][e]) for e in range(NE)]

    def by_feature(w):
        return w.reshape(KD, P, -1).transpose(1, 0, 2).reshape(P, -1)

    w_ffn = np.stack([np.concatenate([by_feature(u), by_feature(g), d], axis=1) for u, g, d in experts])
    consts = np.concatenate([np.eye(P), np.tile(np.arange(NE), (P, 1))], axis=1).astype(np.float32)

    q_sem, k_sem = (a[f"L0_attn_w{n}_sem"].reshape(D, GROUPS, 2 * DS) for n in "qk")
    geo = np.stack([a[f"L0_attn_w{n}_geo"].reshape(D, GROUPS, 2, 2, HALF_G) for n in "qk"], axis=2)
    x1, x2 = (geo[:, :, :, :, j].reshape(D, GROUPS, P) for j in range(2))
    cols = np.concatenate([q_sem, k_sem, x1, x2], axis=2)
    w_qk = np.stack([by_feature(cols[:, g]) for g in range(GROUPS)])
    w_qk = np.concatenate([w_qk, w_qk[:1]])
    w_v = np.stack([by_feature(a["L0_attn_wv"][:, g * 2 * DV:(g + 1) * 2 * DV]) for g in range(GROUPS)])
    w_o = a["L0_attn_wo"].reshape(GROUPS, 2, DV, D).transpose(0, 2, 1, 3).reshape(GROUPS, P, WO)
    inv_freq = (np.float32(1.0) / np.float32(ROPE_BASE) ** (np.arange(HALF_G, dtype=np.float32) / HALF_G))
    angle = np.arange(N, dtype=np.float32)[None, :] * inv_freq.astype(np.float32)[:, None]
    rope = np.stack([np.tile(f(angle.astype(np.float64)), (4, 1)) for f in (np.cos, np.sin)], axis=1)
    return {
        "w_qk": w_qk,
        "w_v": w_v,
        "w_o": w_o,
        "gate": a["L0_attn_gate_logit"].reshape(GROUPS, 2).T,
        "rope": rope.astype(np.float32),
        "x": a["L0_attn_x"].reshape(N, D),
        "w_ffn": w_ffn,
        "w_router": by_feature(a["L0_ffn_router_w"].T),
        "bias": a["L0_ffn_router_bias"],
        "consts": consts,
    }


def kernel(**inputs):
    import concourse.bacc as bacc
    from concourse.bass_utils import run_bass_kernel_spmd

    arrays = {k: np.ascontiguousarray(v) for k, v in layouts({k: np.asarray(v) for k, v in inputs.items()}).items()}
    nc = bacc.Bacc("TRN2", target_bir_lowering=False, num_devices=1)
    aps = {k: nc.dram_tensor(f"in_{k}", v.shape, mybir.dt.from_np(v.dtype), kind="ExternalInput").ap()
           for k, v in arrays.items()}
    out = nc.dram_tensor("out_0", (N, D), F32, kind="ExternalOutput").ap()
    build(nc, {**aps, "out": out})
    r = run_bass_kernel_spmd(nc, [{f"in_{k}": v for k, v in arrays.items()}], core_ids=[0])
    return r.results[0]["out_0"].reshape(1, N, D)
```
